# Optimizing a Trainium2 kernel written in Bass

```python
import numpy as np
import jax
import jax.numpy as jnp

def _softmax(x, axis=-1):
    return jax.nn.softmax(x, axis=axis)

def _gelu(x):
    return jax.nn.gelu(x, approximate=True)

def _silu(x):
    return jax.nn.silu(x)

def _sigmoid(x):
    return jax.nn.sigmoid(x)

def _layernorm(x, axis=-1, eps=1e-05):
    m = jnp.mean(x, axis=axis, keepdims=True)
    v = jnp.var(x, axis=axis, keepdims=True)
    return (x - m) / jnp.sqrt(v + eps)

def _scatter_add(tgt, idx, src, axis=0):
    return tgt.at[idx].add(src)

def _segment_sum(src, seg, n):
    return jax.ops.segment_sum(src, seg, n)
kernel_name = 'mk_adj_preln_d2_adj_r2_6a01e2'

def setup_inputs(seed: int=0):
    np.random.seed(seed)
    _w = jnp.asarray

    def _rec_inputs():
        import jax
        import jax.numpy as jnp
        _gk = jax.random.key(seed)
        x = -0.0005207 + 1.001 * jax.random.normal(jax.random.fold_in(_gk, 1), (8192, 128), jnp.float32)
        _a = jax.random.bernoulli(jax.random.fold_in(_gk, 2), 0.000488281, (8192, 8192))
        _a = jnp.logical_or(_a, jnp.swapaxes(_a, -1, -2))
        _a = jnp.logical_or(_a, jnp.eye(8192, dtype=bool))
        adj = _a.astype(jnp.int32)
        return (x, adj)
    x, adj = _rec_inputs()

    def _L0_gnn_setup():
        import jax, jax.numpy as jnp
        import numpy as np
        ALPHA = 0.2
        NEG_INF = -9000000000000000.0
        key = jax.random.key(seed)
        k1, k2, k3, k4 = jax.random.split(key, 4)
        N, F_in, F_out = (4096, 128, 128)
        x = jax.random.normal(k1, (N, F_in), dtype=jnp.float32)
        adj = jax.random.randint(k2, (N, N), 0, 2, dtype=jnp.int32)
        W = jax.random.normal(k3, (F_in, F_out), dtype=jnp.float32) * (1.0 / np.sqrt(F_in))
        a = jax.random.normal(k4, (2 * F_out, 1), dtype=jnp.float32) * 0.05
        return {'x': x, 'adj': adj, 'W': W, 'a': a}
    _L0_gnn_all = _L0_gnn_setup()
    _L0_gnn_in = {k: v for k, v in _L0_gnn_all.items() if k in ('W', 'a')}
    del _L0_gnn_all

    def _L1_gnn_setup():
        import math
        import jax, jax.numpy as jnp
        import numpy as np
        N = 4096
        F_IN = 128
        F_OUT = 128
        key = jax.random.key(seed)
        ks = jax.random.split(key, 9)
        s = 1.0 / math.sqrt(F_IN)
        return {'x': jax.random.normal(ks[0], (N, F_IN), dtype=jnp.float32), 'adj': jax.random.randint(ks[1], (N, N), 0, 2, dtype=jnp.int32), 'Wq': jax.random.uniform(ks[2], (F_OUT, F_IN), jnp.float32, -s, s), 'bq': jax.random.uniform(ks[3], (F_OUT,), jnp.float32, -s, s), 'Wk': jax.random.uniform(ks[4], (F_OUT, F_IN), jnp.float32, -s, s), 'bk': jax.random.uniform(ks[5], (F_OUT,), jnp.float32, -s, s), 'Wv': jax.random.uniform(ks[6], (F_OUT, F_IN), jnp.float32, -s, s), 'bv': jax.random.uniform(ks[7], (F_OUT,), jnp.float32, -s, s)}
    _L1_gnn_all = _L1_gnn_setup()
    _L1_gnn_in = {k: v for k, v in _L1_gnn_all.items() if k in ('Wq', 'bq', 'Wk', 'bk', 'Wv', 'bv')}
    del _L1_gnn_all
    return {'x': x, 'adj': adj, 'L0_gnn_W': _L0_gnn_in['W'], 'L0_gnn_a': _L0_gnn_in['a'], 'L1_gnn_Wq': _L1_gnn_in['Wq'], 'L1_gnn_bq': _L1_gnn_in['bq'], 'L1_gnn_Wk': _L1_gnn_in['Wk'], 'L1_gnn_bk': _L1_gnn_in['bk'], 'L1_gnn_Wv': _L1_gnn_in['Wv'], 'L1_gnn_bv': _L1_gnn_in['bv']}

def reference(x, adj, L0_gnn_W, L0_gnn_a, L1_gnn_Wq, L1_gnn_bq, L1_gnn_Wk, L1_gnn_bk, L1_gnn_Wv, L1_gnn_bv):
    import jax
    import jax.numpy as jnp

    def _L0_gnn_ref(x, adj, W, a):
        import jax, jax.numpy as jnp
        import numpy as np
        ALPHA = 0.2
        NEG_INF = -9000000000000000.0
        h = x @ W
        F_out = h.shape[1]
        a1 = a[:F_out, 0]
        a2 = a[F_out:, 0]
        s1 = h @ a1
        s2 = h @ a2
        e = jax.nn.leaky_relu(s1[:, None] + s2[None, :], negative_slope=ALPHA)
        scores = jnp.where(adj > 0, e, NEG_INF)
        attention = jax.nn.softmax(scores, axis=1)
        h_prime = attention @ h
        return jax.nn.elu(h_prime)

    def _L1_gnn_ref(x, adj, Wq, bq, Wk, bk, Wv, bv):
        import math
        import jax, jax.numpy as jnp
        import numpy as np
        N = 4096
        F_IN = 128
        F_OUT = 128
        q = x @ Wq.T + bq
        k = x @ Wk.T + bk
        v = x @ Wv.T + bv
        d = q.shape[-1]
        scores = q @ k.T / jnp.sqrt(jnp.asarray(d, q.dtype))
        neg = jnp.asarray(-9000000000000000.0, scores.dtype)
        scores = jnp.where(adj > 0, scores, neg)
        attention = jax.nn.softmax(scores, axis=-1)
        att = attention @ v
        return jax.nn.elu(att)
    h = jnp.maximum(_layernorm(x, axis=-1), 0.0)
    x = x + _L0_gnn_ref(h, adj, L0_gnn_W, L0_gnn_a)
    h = jnp.maximum(_layernorm(x, axis=-1), 0.0)
    x = x + _L1_gnn_ref(h, adj, L1_gnn_Wq, L1_gnn_bq, L1_gnn_Wk, L1_gnn_bk, L1_gnn_Wv, L1_gnn_bv)
    return x

_drawn_inputs = setup_inputs


def setup_inputs(seed=0):
    import zlib

    import numpy as np

    out = dict(_drawn_inputs(seed))
    spreads = {}
    factors = {'L1_gnn_Wq': 4.857, 'L1_gnn_bq': 8.0, 'L1_gnn_Wk': 4.468, 'L1_gnn_bk': 8.0}
    for name, (base, spread) in spreads.items():
        noise = np.random.default_rng([zlib.crc32(name.encode()), seed]).standard_normal(out[name].shape)
        drawn = base * np.exp(spread * noise) if base else spread * noise
        out[name] = jnp.asarray(drawn.astype(out[name].dtype))
    for name, factor in factors.items():
        out[name] = (out[name] * factor).astype(out[name].dtype)
    return out
```

```python
from contextlib import ExitStack

import concourse.bass as bass
from concourse import mybir

P = 128
F32 = mybir.dt.float32
I32 = mybir.dt.int32
ALU = mybir.AluOpType
ACT = mybir.ActivationFunctionType
AX = mybir.AxisListType
NEG = -9000000000000000.0
ALPHA = 0.2
EPS = 1e-05


def two_layer_graph_attention(nc, x, adj, W, a, Wq, bq, Wk, bk, Wv, bv, out):
    N, D = x.shape
    assert D == P and N % 512 == 0
    T = N // P
    PIECE = min(2048, N // 2)
    PIECES = N // PIECE
    CH = 512
    CHUNKS = N // CH
    PER_PIECE = PIECE // CH
    SCALE = float(D) ** -0.5

    x_tiles = x.rearrange("(t p) d -> p t d", p=P)
    out_tiles = out.rearrange("(t p) d -> p t d", p=P)
    col = lambda v: v.rearrange("(p o) -> p o", o=1)

    with ExitStack() as ctx:
        sb = lambda name, shape, dt=F32: ctx.enter_context(nc.sbuf_tensor(name, shape, dt))
        pb = lambda name, shape, dt=F32: ctx.enter_context(nc.psum_tensor(name, shape, dt))
        sem = lambda name: ctx.enter_context(nc.semaphore(name))

        X = sb("X", [P, T, D])
        H = sb("H", [P, T, D])
        HT = sb("HT", [P, N])
        adj_sb = sb("adj_sb", [P, PIECES, PIECE], I32)
        S = sb("S", [P, N])
        penalty = sb("penalty", [P, PIECE])
        PT = sb("PT", [P, 2, CH])
        ident = sb("ident", [P, P])
        weights = sb("weights", [P, 4, D])
        w_sb, wq_sb, wk_sb, wv_sb = (weights[:, n, :] for n in range(4))
        cols = sb("cols", [P, 5])
        a1_c, a2_c, bq_c, bk_c, bv_c = (cols[:, n:n + 1] for n in range(5))
        wT = sb("wT", [P, 2, D])
        bqrep = sb("bqrep", [P, D])
        bvrow = sb("bvrow", [1, D])
        ones = sb("ones", [P, D])
        mix = sb("mix", [P, 2, D])
        proj = sb("proj", [P, 2, D])
        ubias = sb("ubias", [P, 2])
        crow = sb("crow", [P, 2])
        cadd = sb("cadd", [P, 2])
        obias = sb("obias", [P, 2, D])
        eps = sb("eps", [P, 1])
        stats = sb("stats", [P, T, 6])
        mv = sb("mv", [P, T, 2])
        sd = sb("sd", [P, T])
        rstd = sb("rstd", [P, T])
        shift = sb("shift", [P, T])
        UT = sb("UT", [P, P])
        stage = sb("stage", [P, CH // P, D])
        rows = sb("rows", [P, P])
        cbias = sb("cbias", [P, 1])
        pmax = sb("pmax", [P, PIECES])
        nmax = sb("nmax", [P, 1])
        rsum = sb("rsum", [P, 1])
        rrec = sb("rrec", [P, 1])
        AT = sb("AT", [P, P])
        z = sb("z", [P, D])
        zneg = sb("zneg", [P, D])
        zexp = sb("zexp", [P, D])
        zpos = sb("zpos", [P, D])

        psS = pb("psS", [P, 2, CH])
        psT = pb("psT", [P, 2, CH])
        psA = pb("psA", [P, CH])
        psO = pb("psO", [P, CH])
        psU = pb("psU", [P, CH])
        psM = pb("psM", [P, CH])

        consts_in = sem("consts_in")
        bv_in = sem("bv_in")
        x_in = sem("x_in")
        ones_set = sem("ones_set")
        ident_set = sem("ident_set")
        eps_set = sem("eps_set")
        bq_spread = sem("bq_spread")
        w_turned = sem("w_turned")
        w_turned_sb = sem("w_turned_sb")
        mixed = sem("mixed")
        mixed_sb = sem("mixed_sb")
        stats_done = sem("stats_done")
        mv_done = sem("mv_done")
        sd_done = sem("sd_done")
        rstd_done = sem("rstd_done")
        shift_done = sem("shift_done")
        h_done = sem("h_done")
        h_kept = sem("h_kept")
        rows_done = sem("rows_done")
        h_turned = sem("h_turned")
        ht_done = sem("ht_done")
        adj_in = [sem(f"adj_in{q}") for q in range(PIECES)]
        adj_used = [sem(f"adj_used{q}") for q in range(PIECES)]
        u_done = sem("u_done")
        ut_done = sem("ut_done")
        cbias_done = sem("cbias_done")
        s_done = sem("s_done")
        s_moved = sem("s_moved")
        penalty_done = sem("penalty_done")
        leaky_done = sem("leaky_done")
        masked = sem("masked")
        pmax_done = sem("pmax_done")
        nmax_done = sem("nmax_done")
        exp_done = sem("exp_done")
        rrec_done = sem("rrec_done")
        p_turned = sem("p_turned")
        pt_done = sem("pt_done")
        pt_used = sem("pt_used")
        a_done = sem("a_done")
        at_done = sem("at_done")
        o_done = sem("o_done")
        z_done = sem("z_done")
        z2_done = sem("z2_done")
        zneg_done = sem("zneg_done")
        zpos_done = sem("zpos_done")
        zexp_done = sem("zexp_done")
        y_done = sem("y_done")
        x_done = sem("x_done")
        out_written = sem("out_written")

        block = ctx.enter_context(nc.Block())

        def counted(eng, n, body):
            body(0, True)
            with eng.Fori(1, n) as i:
                body(i, False)

        @block.sync
        def _(sp):
            for n, w in enumerate((W, Wq, Wk, Wv)):
                sp.dma_start(weights[:, n, :], w).then_inc(consts_in, 16)
            for n, v in enumerate((a[0:D, :], a[D:2 * D, :], col(bq), col(bk), col(bv))):
                sp.dma_start(cols[:, n:n + 1], v).then_inc(consts_in, 16)
            sp.dma_start(bvrow[:, :], bv.rearrange("(o d) -> o d", o=1)).then_inc(bv_in, 16)
            sp.dma_start(X[:, :, :], x_tiles).then_inc(x_in, 16)
            for layer in range(2):
                def load(i, first):
                    for q in range(PIECES):
                        if layer or not first:
                            sp.wait_ge(adj_used[q], i + layer * T)
                        sp.dma_start(adj_sb[:, q, :], adj[bass.ds(i * P, P), q * PIECE:(q + 1) * PIECE])\
                          .then_inc(adj_in[q], 16)

                counted(sp, T, load)
            sp.wait_ge(x_done, 2 * T)
            sp.dma_start(out_tiles, X[:, :, :]).then_inc(out_written, 16)
            sp.wait_ge(out_written, 16)

        @block.gpsimd
        def _(pool):
            nc.gpsimd.memset(ones[:, :], 1.0).then_inc(ones_set, 1)
            pool.wait_ge(ones_set, 1)
            nc.gpsimd.affine_select(out=ident[:, :], in_=ones[:, :], compare_op=ALU.is_equal, fill=0.0, base=0,
                                    pattern=[[-1, P]], channel_multiplier=1).then_inc(ident_set, 1)
            nc.gpsimd.memset(mix[:, 0, :], 0.0).then_inc(ident_set, 1)
            nc.gpsimd.memset(eps[:, :], EPS).then_inc(eps_set, 1)
            for layer in range(2):
                with pool.Fori(0, CHUNKS) as i:
                    pool.wait_ge(h_done, (i + 1) * (CH // P) + layer * T)
                    nc.gpsimd.tensor_copy(H[:, bass.ds(i * (CH // P), CH // P), :], stage[:, :, :]).then_inc(h_kept, 1)
                pool.wait_ge(ht_done, (layer + 1) * CHUNKS)
                def copy_rows(i, first):
                    if layer or not first:
                        pool.wait_ge(u_done, i + layer * T)
                    nc.gpsimd.tensor_copy(rows[:, :], HT[:, bass.ds(i * P, P)]).then_inc(rows_done, 1)

                counted(pool, T, copy_rows)

        @block.vector
        def _(dve):
            dve.wait_ge(consts_in, 16 * 9)
            dve.wait_ge(ones_set, 1)
            nc.vector.tensor_scalar(bqrep[:, :], ones[:, :], bq_c, None, ALU.mult).then_inc(bq_spread, 1)
            dve.wait_ge(w_turned, 2)
            nc.vector.tensor_copy(wT[:, :, :], psT[:, 0, 0:2 * D].rearrange("p (n d) -> p n d", n=2))\
              .then_inc(w_turned_sb, 1)
            dve.wait_ge(mixed, 1)
            nc.vector.tensor_copy(ubias[:, 0:1], psM[:, 0:1]).then_inc(mixed_sb, 1)
            nc.vector.tensor_copy(crow[:, 0:1], psM[:, 1:2]).then_inc(mixed_sb, 1)
            nc.vector.tensor_copy(ubias[:, 1:2], psM[:, 2:3]).then_inc(mixed_sb, 1)
            nc.vector.tensor_copy(crow[:, 1:2], psM[:, 3:4]).then_inc(mixed_sb, 1)
            nc.vector.memset(cadd[:, 0:1], 0.0).then_inc(mixed_sb, 1)
            nc.vector.tensor_copy(cadd[:, 1:2], psM[:, 4:5]).then_inc(mixed_sb, 1)
            nc.vector.tensor_copy(mix[:, 1, :], psM[:, 128:256]).then_inc(mixed_sb, 1)
            nc.vector.memset(obias[:, 0, :], 0.0).then_inc(mixed_sb, 1)
            nc.vector.tensor_copy(obias[:, 1, :], psM[:, 256:384]).then_inc(mixed_sb, 1)
            nc.vector.tensor_copy(proj[:, 0, :], w_sb).then_inc(mixed_sb, 1)
            nc.vector.tensor_copy(proj[:, 1, :], wT[:, 1, :]).then_inc(mixed_sb, 1)

            for layer in range(2):
                base = layer * T
                if layer == 0:
                    dve.wait_ge(x_in, 16)
                else:
                    dve.wait_ge(x_done, T)
                with dve.Fori(0, T) as i:
                    nc.vector.bn_stats(stats[:, bass.ds(i, 1), :], X[:, bass.ds(i, 1), :]).then_inc(stats_done, 1)
                dve.wait_ge(stats_done, base + T)
                for t in range(T):
                    nc.vector.bn_aggr(mv[:, t, :], stats[:, t, :]).then_inc(mv_done, 1)
                dve.wait_ge(sd_done, layer + 1)
                nc.vector.reciprocal(rstd[:, :], sd[:, :]).then_inc(rstd_done, 1)
                dve.wait_ge(rstd_done, layer + 1)
                nc.vector.scalar_tensor_tensor(out=shift[:, :], in0=mv[:, :, 0], scalar=-1.0, in1=rstd[:, :],
                                               op0=ALU.mult, op1=ALU.mult).then_inc(shift_done, 1)
                with dve.Fori(0, CHUNKS) as i:
                    dve.wait_ge(h_turned, i + 1 + layer * CHUNKS)
                    nc.vector.tensor_copy(HT[:, bass.ds(i * CH, CH)], psT[:, 0, :]).then_inc(ht_done, 1)

                with dve.Fori(0, T) as i:
                    t = i + base
                    dve.wait_ge(u_done, t + 1)
                    nc.vector.tensor_scalar(cbias[:, :], psM[:, 0:1], cadd[:, layer:layer + 1],
                                            1.0 if layer == 0 else SCALE, ALU.add, ALU.mult).then_inc(cbias_done, 1)
                    for q in range(PIECES):
                        piece = S[:, q * PIECE:(q + 1) * PIECE]
                        dve.wait_ge(s_moved, CHUNKS * t + (q + 1) * PER_PIECE)
                        if layer == 0:
                            nc.vector.scalar_tensor_tensor(out=piece, in0=piece, scalar=ALPHA, in1=piece,
                                                           op0=ALU.mult, op1=ALU.max).then_inc(leaky_done, 1)
                        if q:
                            dve.wait_ge(masked, PIECES * t + q)
                        dve.wait_ge(adj_in[q], 16 * t + 16)
                        nc.vector.tensor_scalar(penalty[:, :], adj_sb[:, q, :], 0.0, NEG, ALU.is_le, ALU.mult)\
                          .then_inc(penalty_done, 1)
                        if layer == 0:
                            dve.wait_ge(leaky_done, PIECES * t + q + 1)
                        dve.wait_ge(penalty_done, PIECES * t + q + 1)
                        dve.sem_inc(adj_used[q], 1)
                        nc.vector.tensor_tensor_reduce(out=piece, in0=piece, in1=penalty[:, :], scale=1.0,
                                                       scalar=-3.0e38, op0=ALU.add, op1=ALU.max,
                                                       accum_out=pmax[:, q:q + 1]).then_inc(masked, 1)
                    dve.wait_ge(masked, PIECES * t + PIECES)
                    nc.vector.tensor_reduce(nmax[:, :], pmax[:, :], AX.X, ALU.max).then_inc(pmax_done, 1)
                    dve.wait_ge(pmax_done, t + 1)
                    nc.vector.tensor_scalar(nmax[:, :], nmax[:, :], -1.0, None, ALU.mult).then_inc(nmax_done, 1)
                    dve.wait_ge(exp_done, t + 1)
                    nc.vector.reciprocal(rrec[:, :], rsum[:, :]).then_inc(rrec_done, 1)
                    dve.wait_ge(a_done, t + 1)
                    nc.vector.tensor_copy(AT[:, :], psA[:, 0:P]).then_inc(at_done, 1)
                    dve.wait_ge(rrec_done, t + 1)
                    dve.wait_ge(o_done, t + 1)
                    nc.vector.scalar_tensor_tensor(out=z[:, :], in0=psO[:, 0:D], scalar=rrec[:, 0:1],
                                                   in1=obias[:, layer, :], op0=ALU.mult, op1=ALU.add).then_inc(z_done, 1)
                    dve.wait_ge(z_done, t + 1)
                    nc.vector.tensor_scalar(zneg[:, :], z[:, :], 0.0, None, ALU.min).then_inc(zneg_done, 1)
                    nc.vector.tensor_scalar(zpos[:, :], z[:, :], 0.0, -1.0, ALU.max, ALU.add).then_inc(zpos_done, 1)
                    dve.wait_ge(zexp_done, t + 1)
                    dve.wait_ge(zpos_done, t + 1)
                    nc.vector.tensor_tensor(zpos[:, :], zpos[:, :], zexp[:, :], ALU.add).then_inc(y_done, 1)
                    dve.wait_ge(y_done, t + 1)
                    nc.vector.tensor_tensor(X[:, bass.ds(i, 1), :], X[:, bass.ds(i, 1), :],
                                            zpos[:, :].rearrange("p (o d) -> p o d", o=1), ALU.add).then_inc(x_done, 1)

        @block.scalar
        def _(act):
            act.wait_ge(eps_set, 1)
            act.wait_ge(mixed_sb, 11)
            for layer in range(2):
                base = layer * T
                act.wait_ge(mv_done, base + T)
                nc.scalar.activation(sd[:, :], mv[:, :, 1], ACT.Sqrt, bias=eps[:, 0:1]).then_inc(sd_done, 1)
                act.wait_ge(shift_done, layer + 1)
                def stage_rows(i, first):
                    if layer or not first:
                        act.wait_ge(h_kept, i + layer * CHUNKS)
                        act.wait_ge(h_turned, i + layer * CHUNKS)
                    for n in range(CH // P):
                        m = i * (CH // P) + n
                        nc.scalar.activation(stage[:, n:n + 1, :], X[:, bass.ds(m, 1), :], ACT.Relu,
                                             bias=shift[:, bass.ds(m, 1)], scale=rstd[:, bass.ds(m, 1)])\
                          .then_inc(h_done, 1)

                counted(act, CHUNKS, stage_rows)
                with act.Fori(0, T) as i:
                    t = i + base
                    act.wait_ge(u_done, t + 1)
                    nc.scalar.activation(UT[:, :], psU[:, 0:P], ACT.Identity, bias=ubias[:, layer:layer + 1])\
                      .then_inc(ut_done, 1)
                    act.wait_ge(cbias_done, t + 1)
                    for c in range(CHUNKS):
                        act.wait_ge(s_done, CHUNKS * t + c + 1)
                        nc.scalar.activation(S[:, c * CH:(c + 1) * CH], psS[:, c % 2, :], ACT.Identity,
                                             bias=cbias[:, 0:1], scale=1.0 if layer == 0 else SCALE).then_inc(s_moved, 1)
                    act.wait_ge(nmax_done, t + 1)
                    nc.scalar.activation(S[:, :], S[:, :], ACT.Exp, bias=nmax[:, 0:1], accum_out=rsum[:, 0:1])\
                      .then_inc(exp_done, 1)
                    for c in range(CHUNKS):
                        act.wait_ge(p_turned, CHUNKS * t + c + 1)
                        if c >= 2:
                            act.wait_ge(pt_used, CHUNKS * t + c - 1)
                        nc.scalar.activation(PT[:, c % 2, :], psT[:, c % 2, :], ACT.Identity).then_inc(pt_done, 1)
                    act.wait_ge(zneg_done, t + 1)
                    nc.scalar.activation(zexp[:, :], zneg[:, :], ACT.Exp).then_inc(zexp_done, 1)

        @block.tensor
        def _(pe):
            pe.wait_ge(consts_in, 16 * 9)
            pe.wait_ge(ident_set, 2)
            pe.wait_ge(bv_in, 16)
            nc.tensor.transpose(psT[:, 0, 0:D], w_sb, ident[:, :]).then_inc(w_turned, 1)
            nc.tensor.transpose(psT[:, 0, D:2 * D], wv_sb, ident[:, :]).then_inc(w_turned, 1)
            pe.wait_ge(w_turned_sb, 1)
            pe.wait_ge(bq_spread, 1)
            nc.tensor.matmul(psM[:, 0:1], wT[:, 0, :], a2_c, start=True, stop=True)
            nc.tensor.matmul(psM[:, 1:2], wT[:, 0, :], a1_c, start=True, stop=True)
            nc.tensor.matmul(psM[:, 2:3], wk_sb, bq_c, start=True, stop=True)
            nc.tensor.matmul(psM[:, 3:4], wq_sb, bk_c, start=True, stop=True)
            nc.tensor.matmul(psM[:, 4:5], bqrep[:, :], bk_c, start=True, stop=True)
            nc.tensor.matmul(psM[:, 128:256], wq_sb, wk_sb, start=True, stop=True)
            nc.tensor.matmul(psM[:, 256:384], ones[0:1, :], bvrow[:, :], start=True, stop=True).then_inc(mixed, 1)
            pe.wait_ge(mixed_sb, 11)
            for layer in range(2):
                base = layer * T
                def turn_rows(i, first):
                    pe.wait_ge(h_done, (i + 1) * (CH // P) + base)
                    if layer or not first:
                        pe.wait_ge(ht_done, i + layer * CHUNKS)
                    for n in range(CH // P):
                        last = nc.tensor.transpose(psT[:, 0, n * P:(n + 1) * P],
                                                   stage[:, n, :], ident[:, :])
                    last.then_inc(h_turned, 1)

                counted(pe, CHUNKS, turn_rows)
                pe.wait_ge(ht_done, (layer + 1) * CHUNKS)
                pe.wait_ge(h_kept, (layer + 1) * CHUNKS)
                with pe.Fori(0, T) as i:
                    t = i + base
                    pe.wait_ge(rows_done, t + 1)
                    nc.tensor.matmul(psU[:, 0:P], mix[:, layer, :], rows[:, :], start=True, stop=True)
                    nc.tensor.matmul(psM[:, 0:1], rows[:, :], crow[:, layer:layer + 1], start=True, stop=True)\
                      .then_inc(u_done, 1)
                    pe.wait_ge(ut_done, t + 1)
                    for c in range(CHUNKS):
                        if c >= 2:
                            pe.wait_ge(s_moved, CHUNKS * t + c - 1)
                        nc.tensor.matmul(psS[:, c % 2, :], UT[:, :], HT[:, c * CH:(c + 1) * CH], start=True, stop=True)\
                          .then_inc(s_done, 1)
                    pe.wait_ge(exp_done, t + 1)

                    def weigh(c):
                        pe.wait_ge(pt_done, CHUNKS * t + c + 1)
                        for n in range(CH // P):
                            last = nc.tensor.matmul(psA[:, 0:P], H[:, c * (CH // P) + n, :], PT[:, c % 2, n * P:(n + 1) * P],
                                                    start=(c == 0 and n == 0), stop=(c == CHUNKS - 1 and n == CH // P - 1))
                        last.then_inc(pt_used, 1)
                        return last

                    for c in range(CHUNKS):
                        if c >= 2:
                            pe.wait_ge(pt_done, CHUNKS * t + c - 1)
                        for n in range(CH // P):
                            at = c * CH + n * P
                            last = nc.tensor.transpose(psT[:, c % 2, n * P:(n + 1) * P], S[:, at:at + P], ident[:, :])
                        last.then_inc(p_turned, 1)
                        if c >= 1:
                            weigh(c - 1)
                    weigh(CHUNKS - 1)
                    pe.wait_ge(pt_used, CHUNKS * t + CHUNKS)
                    pe.sem_inc(a_done, 1)
                    pe.wait_ge(at_done, t + 1)
                    nc.tensor.matmul(psO[:, 0:D], AT[:, :], proj[:, layer, :], start=True, stop=True).then_inc(o_done, 1)


_INS = ['x', 'adj', 'L0_gnn_W', 'L0_gnn_a', 'L1_gnn_Wq', 'L1_gnn_bq', 'L1_gnn_Wk', 'L1_gnn_bk', 'L1_gnn_Wv', 'L1_gnn_bv']
_OUTS = [((8192, 128), 'float32')]


def kernel(**inputs):
    import numpy as _np
    import concourse.bacc as _bacc
    from concourse import mybir as _mybir
    from concourse.bass_utils import run_bass_kernel_spmd as _run

    nc = _bacc.Bacc("TRN2", target_bir_lowering=False, num_devices=1)
    arrays, args = {}, []
    for name in _INS:
        a = _np.ascontiguousarray(inputs[name])
        arrays[f"in_{name}_dram"] = a
        args.append(nc.dram_tensor(f"in_{name}_dram", a.shape, _mybir.dt.from_np(a.dtype), kind="ExternalInput").ap())
    for i, (shape, dtype) in enumerate(_OUTS):
        dt = _mybir.dt.from_np(_np.dtype(dtype))
        args.append(nc.dram_tensor(f"out_{i}_dram", shape, dt, kind="ExternalOutput").ap())
    two_layer_graph_attention(nc, *args)
    r = _run(nc, [arrays], core_ids=[0])
    return r.results[0]["out_0_dram"]
```

```python
from contextlib import ExitStack

import concourse.bass as bass
from concourse import mybir

P = 128
F32 = mybir.dt.float32
F16 = mybir.dt.float16
BF16 = mybir.dt.bfloat16
I32 = mybir.dt.int32
U32 = mybir.dt.uint32
ALU = mybir.AluOpType
ACT = mybir.ActivationFunctionType
AX = mybir.AxisListType
NEG = -9000000000000000.0
ALPHA = 0.2
EPS = 1e-05

SEGS = 14
PLACE_BITS = 10
EXACT = 2 ** 24
WORDS = 24
DEPTH = 3
SLOTS = 24
CHUNKS = 10
GROUP = 4
QUARTERS = 4


def two_layer_graph_attention(nc, x, adj, W, a, Wq, bq, Wk, bk, Wv, bv, out):
    N, D = x.shape
    assert D == P and N % (2 * GROUP * P) == 0
    T = N // P
    G = T // GROUP
    SCALE = float(D) ** -0.5
    DE = D + 1
    QCOLS = CHUNKS * P
    BLOCK = -(-N // SEGS)
    QUARTER = N // QUARTERS
    assert BLOCK < 2 ** PLACE_BITS and SEGS + PLACE_BITS <= 24

    x_tiles = x.rearrange("(t p) d -> p t d", p=P)
    out_tiles = out.rearrange("(t p) d -> p t d", p=P)
    col = lambda v: v.rearrange("(p o) -> p o", o=1)
    tables = [nc.dram_tensor(f"table{n}", [N, D], F32, kind="Internal").ap() for n in range(2)]

    with ExitStack() as ctx:
        ARENA = 53000
        arena = ctx.enter_context(nc.sbuf_tensor("arena", [P, ARENA], F32))
        psum = ctx.enter_context(nc.psum_tensor("psum", [P, 8, 512], F32))
        sem = lambda name: ctx.enter_context(nc.semaphore(name))

        top = [0]

        def place(shape, dt=F32):
            count = 1
            for n in shape:
                count *= n
            words = -(-count * (2 if dt in (BF16, F16) else 4) // 4)
            words += words % 2
            v = arena[:, top[0]:top[0] + words]
            top[0] += words
            assert top[0] <= ARENA, top
            if dt != F32:
                v = v.bitcast(dt)
            v = v[:, 0:count]
            names = "abcd"[:len(shape)]
            if len(shape) > 1:
                v = v.rearrange(f"p ({' '.join(names)}) -> p {' '.join(names)}",
                                **{k: n for k, n in zip(names, shape)})
            return v

        X = place([T, D])
        ident = place([P])
        ones = place([DE])
        weights = place([4, D])
        w_sb, wq_sb, wk_sb, wv_sb = (weights[:, n, :] for n in range(4))
        wk_bk = place([DE])
        cols = place([4])
        a1_c, a2_c, bq_c, bk_c = (cols[:, n:n + 1] for n in range(4))
        bvrow = place([D])
        wT = place([2, D])
        spread = place([2, D])
        mix = place([2, DE])
        mix_bias = place([2, DE])
        mix_col = place([2])
        proj = place([2, D])
        obias = place([2, D])
        eps = place([1])
        stats = place([T, 6])
        half_gap = place([T])
        mean = place([T])
        var = place([T])
        sd = place([T])
        rstd = place([T])
        shift = place([T])
        bad = place([4])
        bad_row = place([1])
        flag = place([1], I32)
        common = top[0]

        U = place([T, DE])
        idx_all = place([T, CHUNKS], U32)
        owner_all = place([T, CHUNKS])
        slot_all = place([T, CHUNKS])
        count_all = place([T])
        sum_all = place([T, QUARTERS])
        end_all = place([T])
        widest_all = place([T])
        iota_q = place([CHUNKS])
        iota_slot = place([SLOTS])
        iota_row = place([P])
        iota_row16 = place([P], BF16)
        ident16 = place([P], BF16)
        lists = top[0]

        stage = place([2, GROUP, D])
        stageT = place([2, GROUP * P])
        adj_sb = place([QUARTERS, QUARTER], I32)
        mask = place([2, SEGS * BLOCK], BF16)
        shifted = place([SEGS, P], BF16)
        upto = place([P], BF16)
        ones16 = place([P], BF16)
        place_hi = place([BLOCK + 64], BF16)
        place_lo = place([BLOCK + 64], BF16)
        scratch = place([QCOLS], F32)
        iota16 = place([QCOLS], F16)
        rest = place([2, BLOCK])
        words = place([GROUP, WORDS])
        words_i = place([GROUP * WORDS], I32)
        place_i = place([GROUP * WORDS], I32)
        bits_i = place([GROUP * WORDS], I32)
        place_f = place([GROUP * WORDS])
        bits_f = place([DEPTH, GROUP * WORDS])
        top_f = place([DEPTH, GROUP * WORDS])
        expo_i = place([DEPTH, GROUP * WORDS], I32)
        node_f = place([DEPTH, GROUP * WORDS])
        found = place([DEPTH, GROUP, WORDS])
        found2 = place([2, DEPTH * WORDS])
        listed = place([GROUP, SLOTS + 1])
        is_listed = place([GROUP, SLOTS])
        count4 = place([GROUP])
        count16 = place([GROUP], BF16)
        end4 = place([GROUP])
        listed_i = place([GROUP * (SLOTS + 1)], I32)
        lo_i = place([GROUP * (SLOTS + 1)], I32)
        hi16 = place([GROUP, SLOTS + 2], BF16)
        lo16 = place([GROUP, SLOTS + 2], BF16)
        from_pre = place([QCOLS], BF16)
        from_end = place([QCOLS], BF16)
        mine = place([2, QCOLS], BF16)
        one_hot = place([CHUNKS, SLOTS])
        picked = place([CHUNKS, SLOTS])
        node_q = place([CHUNKS])
        past_q = place([CHUNKS])

        top[0] = lists
        top[0] += 4 * GROUP * P
        idx_now = place([GROUP, CHUNKS], U32)
        Gt = place([GROUP, CHUNKS, DE])
        owned = place([GROUP, CHUNKS, P], BF16)
        owners = place([GROUP, CHUNKS, P])
        owners16 = place([GROUP, CHUNKS, P], BF16)
        weighted = place([2, CHUNKS, P])
        slot_hot = place([GROUP, CHUNKS, SLOTS], BF16)
        slot_e = place([2, CHUNKS, SLOTS], BF16)
        score16 = place([2, CHUNKS], BF16)
        max16 = place([2], BF16)
        prod = place([CHUNKS, DE])
        raw = place([CHUNKS])
        score = place([2, CHUNKS])
        pad = place([SLOTS])
        by_slot = place([SLOTS])
        row_max = place([1])
        gap = place([CHUNKS])
        prob = place([CHUNKS])
        rsum = place([1])
        acc = place([P])
        accT = place([P])
        z = place([D])
        zneg = place([D])
        zexp = place([D])
        y = place([D])

        top[0] = common
        wH = place([T, D])
        wHT = place([N])
        wadj = place([QUARTERS, QUARTER], I32)
        wS = place([N])
        penalty = place([QUARTER])
        wPT = place([2, 512])
        wstage = place([GROUP, D])
        wrows = place([P])
        wUT = place([P])
        wcbias = place([1])
        wpmax = place([QUARTERS])
        wnmax = place([1])
        wrsum = place([1])
        wrrec = place([1])
        wAT = place([P])
        wz = place([D])
        wzneg = place([D])
        wzexp = place([D])
        wzpos = place([D])

        bank = lambda n: psum[:, n, :]
        parts = [(s, min(s + 512, BLOCK)) for s in range(0, BLOCK, 512)]
        V = [psum[:, 2 * v:2 * v + 2, :].rearrange("p a b -> p (a b)")[:, 0:BLOCK] for v in range(2)]
        q_lists = [bank(4 + v)[:, 0:CHUNKS * (SLOTS + 2)].rearrange("p (c k) -> p c k", c=CHUNKS) for v in range(2)]

        turned_ps = [bank(u)[:, 0:CHUNKS // 2 * P // 2].bitcast(BF16) for u in range(2)]

        consts_in = sem("consts_in")
        x_in = sem("x_in")
        pool_consts = sem("pool_consts")
        dve_consts = sem("dve_consts")
        spread_done = sem("spread_done")
        w_turned = sem("w_turned")
        w_turned_sb = sem("w_turned_sb")
        mixed = sem("mixed")
        mixed_sb = sem("mixed_sb")
        stats_done = sem("stats_done")
        gap_done = sem("gap_done")
        mean_done = sem("mean_done")
        var_done = sem("var_done")
        sd_done = sem("sd_done")
        rstd_done = sem("rstd_done")
        shift_done = sem("shift_done")
        h_done = sem("h_done")
        h_turned = sem("h_turned")
        ht_done = sem("ht_done")
        u_out = sem("u_out")
        u_done = sem("u_done")
        u_kept = sem("u_kept")
        table_written = [sem(f"table_written{k}") for k in range(2)]
        adj_in = [sem(f"adj_in{q}") for q in range(QUARTERS)]
        mask_done = sem("mask_done")
        packed = sem("packed")
        top_done = sem("top_done")
        rest_done = sem("rest_done")
        decoded = sem("decoded")
        ltop_done = sem("ltop_done")
        lrest_done = sem("lrest_done")
        count_done = sem("count_done")
        ends_done = sem("ends_done")
        split_done = sem("split_done")
        sel_ready = sem("sel_ready")
        mine_done = sem("mine_done")
        q_done = sem("q_done")
        pick_done = sem("pick_done")
        lists_done = sem("lists_done")
        bad_done = sem("bad_done")
        bad_summed = sem("bad_summed")
        flag_done = sem("flag_done")
        idx_done = sem("idx_done")
        gathering = sem("gathering")
        rows_in = [sem(f"rows_in{b}") for b in range(GROUP)]
        owned_done = sem("owned_done")
        hot_done = sem("hot_done")
        turned = sem("turned")
        owners_done = sem("owners_done")
        spread_u = sem("spread_u")
        prod_done = sem("prod_done")
        raw_done = sem("raw_done")
        score_done = sem("score_done")
        slot_e_done = sem("slot_e_done")
        pad_done = sem("pad_done")
        scattered = sem("scattered")
        by_slot_done = sem("by_slot_done")
        max_done = sem("max_done")
        max_spread = sem("max_spread")
        below_done = sem("below_done")
        prob_done = sem("prob_done")
        weighted_done = sem("weighted_done")
        acc_done = sem("acc_done")
        rsum_done = sem("rsum_done")
        acc_sb = sem("acc_sb")
        acc_turned = sem("acc_turned")
        accT_sb = sem("accT_sb")
        o_done = sem("o_done")
        z_done = sem("z_done")
        zneg_done = sem("zneg_done")
        zexp_done = sem("zexp_done")
        y_done = sem("y_done")
        x_done = sem("x_done")
        out_written = sem("out_written")
        w_h_done = sem("w_h_done")
        w_h_kept = sem("w_h_kept")
        w_rows_done = sem("w_rows_done")
        w_h_turned = sem("w_h_turned")
        w_ht_done = sem("w_ht_done")
        w_adj_in = [sem(f"w_adj_in{q}") for q in range(QUARTERS)]
        w_adj_used = [sem(f"w_adj_used{q}") for q in range(QUARTERS)]
        w_u_done = sem("w_u_done")
        w_ut_done = sem("w_ut_done")
        w_cbias_done = sem("w_cbias_done")
        w_s_done = sem("w_s_done")
        w_s_moved = sem("w_s_moved")
        w_penalty_done = sem("w_penalty_done")
        w_leaky_done = sem("w_leaky_done")
        w_masked = sem("w_masked")
        w_pmax_done = sem("w_pmax_done")
        w_nmax_done = sem("w_nmax_done")
        w_exp_done = sem("w_exp_done")
        w_rrec_done = sem("w_rrec_done")
        w_p_turned = sem("w_p_turned")
        w_pt_done = sem("w_pt_done")
        w_pt_used = sem("w_pt_used")
        w_a_done = sem("w_a_done")
        w_at_done = sem("w_at_done")
        w_o_done = sem("w_o_done")
        w_z_done = sem("w_z_done")
        w_zneg_done = sem("w_zneg_done")
        w_zpos_done = sem("w_zpos_done")
        w_zexp_done = sem("w_zexp_done")
        w_y_done = sem("w_y_done")
        w_x_done = sem("w_x_done")
        w_moments = sem("w_moments")

        WCH = 512
        WCHUNKS = N // WCH
        PER_QUARTER = max(QUARTER // WCH, 1)
        WTILES = WCH // P
        wpsS = [bank(0), bank(1)]
        wpsT = [bank(2), bank(3)]

        block = ctx.enter_context(nc.Block())

        def groups(eng, body):
            body(0, True, G == 1)
            if G > 2:
                with eng.Fori(1, G - 1) as g:
                    body(g, False, False)
            if G > 1:
                body(G - 1, False, True)

        def counted(eng, n, body):
            body(0, True)
            with eng.Fori(1, n) as i:
                body(i, False)

        def in_pairs(eng, body):
            body(0, True, G == 2)
            if G > 4:
                with eng.Fori(1, G // 2 - 1) as j:
                    body(j, False, False)
            if G > 2:
                body(G // 2 - 1, False, True)

        @block.sync
        def _(sp):
            for n, w in enumerate((W, Wq, Wk, Wv)):
                sp.dma_start(weights[:, n, :], w).then_inc(consts_in, 16)
            for n, v in enumerate((a[0:D, :], a[D:2 * D, :], col(bq), col(bk))):
                sp.dma_start(cols[:, n:n + 1], v).then_inc(consts_in, 16)
            sp.dma_start(bvrow[0:1, :], bv.rearrange("(o d) -> o d", o=1)).then_inc(consts_in, 16)
            sp.dma_start(X[:, :, :], x_tiles).then_inc(x_in, 16)

            def write_table(layer):
                with sp.Fori(0, G // 2) as j:
                    for k in range(2):
                        sp.wait_ge(h_done, (2 * j + k + 1) * GROUP + layer * T)
                        sp.dma_start(tables[layer].rearrange("(t p) d -> p t d", p=P)[:, bass.ds((2 * j + k) * GROUP, GROUP), :],
                                     stage[:, k, :, :]).then_inc(table_written[k], 16)

            def load_adj(t, q):
                sp.dma_start(adj_sb[:, q, :], adj[bass.ds(t * P, P), q * QUARTER:(q + 1) * QUARTER])\
                  .then_inc(adj_in[q], 16)

            for q in range(QUARTERS):
                load_adj(0, q)
            write_table(0)
            with sp.Fori(1, T) as t:
                for q in range(QUARTERS):
                    sp.wait_ge(mask_done, QUARTERS * t - QUARTERS + q + 1)
                    load_adj(t, q)

            sp.wait_ge(flag_done, 1)
            whole = sp.value_load(flag[0:1, 0:1], min_val=0, max_val=1)
            with sp.If(whole > 0):
                for layer in range(2):
                    def load_whole(t, first):
                        for q in range(QUARTERS):
                            if layer or not first:
                                sp.wait_ge(w_adj_used[q], t + layer * T)
                            sp.dma_start(wadj[:, q, :], adj[bass.ds(t * P, P), q * QUARTER:(q + 1) * QUARTER])\
                              .then_inc(w_adj_in[q], 16)

                    counted(sp, T, load_whole)
                sp.wait_ge(w_x_done, 2 * T)
                sp.dma_start(out_tiles, X[:, :, :]).then_inc(out_written, 16)
                sp.wait_ge(out_written, 16)
            with sp.Else():
                write_table(1)
                with sp.Fori(0, G) as g:
                    sp.wait_ge(x_done, (g + 1) * GROUP + T)
                    sp.dma_start(out_tiles[:, bass.ds(g * GROUP, GROUP), :], X[:, bass.ds(g * GROUP, GROUP), :])\
                      .then_inc(out_written, 16)
                sp.wait_ge(out_written, 16 * G)

        @block.gpsimd
        def _(pool):
            nc.gpsimd.memset(ones[:, :], 1.0).then_inc(pool_consts, 1)
            pool.wait_ge(pool_consts, 1)
            nc.gpsimd.affine_select(out=ident[:, :], in_=ones[:, 0:P], compare_op=ALU.is_equal, fill=0.0, base=0,
                                    pattern=[[-1, P]], channel_multiplier=1).then_inc(pool_consts, 1)
            nc.gpsimd.affine_select(out=rest[:, 0, 0:P] if BLOCK >= P else scratch[:, 0:P], in_=ones[:, 0:P],
                                    compare_op=ALU.is_ge, fill=0.0, base=0,
                                    pattern=[[1, P]], channel_multiplier=-1).then_inc(pool_consts, 1)
            pool.wait_ge(pool_consts, 3)
            nc.gpsimd.tensor_copy(upto[:, :], rest[:, 0, 0:P] if BLOCK >= P else scratch[:, 0:P]).then_inc(pool_consts, 1)
            nc.gpsimd.memset(eps[:, :], EPS).then_inc(pool_consts, 1)
            nc.gpsimd.memset(ones16[:, :], 1.0).then_inc(pool_consts, 1)
            nc.gpsimd.memset(mix[:, 0, :], 0.0).then_inc(pool_consts, 1)
            nc.gpsimd.memset(mix_bias[:, 0, :], 0.0).then_inc(pool_consts, 1)
            nc.gpsimd.memset(obias[:, 0, :], 0.0).then_inc(pool_consts, 1)
            nc.gpsimd.memset(mask[:, :, N:SEGS * BLOCK] if SEGS * BLOCK > N else mask[:, :, 0:1], 0.0)\
              .then_inc(pool_consts, 1)
            small = dict(channel_multiplier=0, allow_small_or_imprecise_dtypes=True)
            nc.gpsimd.iota(iota_slot[:, :], pattern=[[1, SLOTS]], base=0, **small).then_inc(pool_consts, 1)
            nc.gpsimd.iota(iota_row[:, :], pattern=[[1, P]], base=1, **small).then_inc(pool_consts, 1)
            nc.gpsimd.iota(iota_q[:, :], pattern=[[P, CHUNKS]], base=0, channel_multiplier=1,
                           allow_small_or_imprecise_dtypes=True).then_inc(pool_consts, 1)
            pool.wait_ge(pool_consts, 4)
            nc.gpsimd.iota(scratch[:, :], pattern=[[1, QCOLS]], base=0, **small).then_inc(pool_consts, 1)
            pool.wait_ge(pool_consts, 14)
            nc.gpsimd.tensor_copy(iota16[:, :], scratch[:, :]).then_inc(pool_consts, 1)
            B64 = BLOCK // 64 + 1
            pool.wait_ge(pool_consts, 15)
            nc.gpsimd.iota(scratch[:, 0:64 * B64], pattern=[[64, B64], [0, 64]], base=0, **small).then_inc(pool_consts, 1)
            pool.wait_ge(pool_consts, 16)
            nc.gpsimd.tensor_copy(place_hi[:, 0:BLOCK], scratch[:, 0:BLOCK]).then_inc(pool_consts, 1)
            pool.wait_ge(pool_consts, 17)
            nc.gpsimd.iota(scratch[:, 0:64 * B64], pattern=[[0, B64], [1, 64]], base=0, **small).then_inc(pool_consts, 1)
            pool.wait_ge(pool_consts, 18)
            nc.gpsimd.tensor_copy(place_lo[:, 0:BLOCK], scratch[:, 0:BLOCK]).then_inc(pool_consts, 1)
            pool.wait_ge(pool_consts, 19)
            nc.gpsimd.iota(scratch[:, 0:1], pattern=[[0, 1]], base=1, channel_multiplier=1,
                           allow_small_or_imprecise_dtypes=True).then_inc(pool_consts, 1)
            pool.wait_ge(pool_consts, 20)
            for b in range(GROUP):
                nc.gpsimd.tensor_copy(hi16[:, b, SLOTS + 1:SLOTS + 2], scratch[:, 0:1]).then_inc(pool_consts, 1)
                nc.gpsimd.memset(lo16[:, b, SLOTS + 1:SLOTS + 2], 0.0).then_inc(pool_consts, 1)

            pool.wait_ge(flag_done, 1)
            whole = pool.value_load(flag[0:1, 0:1], min_val=0, max_val=1)
            with pool.If(whole > 0):
                for layer in range(2):
                    with pool.Fori(0, WCHUNKS) as i:
                        pool.wait_ge(w_h_done, (i + 1) * WTILES + layer * T)
                        nc.gpsimd.tensor_copy(wH[:, bass.ds(i * WTILES, WTILES), :], wstage[:, :, :]).then_inc(w_h_kept, 1)
                    pool.wait_ge(w_ht_done, (layer + 1) * WCHUNKS)
                    def copy_rows(i, first):
                        if layer or not first:
                            pool.wait_ge(w_u_done, i + layer * T)
                        nc.gpsimd.tensor_copy(wrows[:, :], wHT[:, bass.ds(i * P, P)]).then_inc(w_rows_done, 1)

                    counted(pool, T, copy_rows)
            with pool.Else():
                nc.gpsimd.memset(Gt[:, :, :, :], 1.0).then_inc(pool_consts, 1)
                pool.wait_ge(pool_consts, 21 + 2 * GROUP)
                for layer in range(2):
                    for k in range(2):
                        pool.wait_ge(table_written[k], 8 * G * (layer + 1))

                    def gather_group(g, first, last, layer=layer):
                        for b in range(GROUP):
                            tt = g * GROUP + b + layer * T
                            if not (first and layer == 0):
                                pool.wait_ge(acc_done, tt - GROUP + 1)
                            nc.gpsimd.tensor_copy(idx_now[:, b:b + 1, :], idx_all[:, bass.ds(g * GROUP + b, 1), :])\
                              .then_inc(idx_done, 1)
                            pool.wait_ge(idx_done, tt + 1)
                            pool.sem_inc(gathering, 1)
                            for c in range(CHUNKS):
                                pool.indirect_dma_start(Gt[:, b, c, 0:D], None, tables[layer],
                                                        bass.IndirectOffsetOnAxis(idx_now[:, b, c:c + 1], 0),
                                                        bounds_check=N - 1, oob_is_err=False).then_inc(rows_in[b], 16)

                    groups(pool, gather_group)

        @block.vector
        def _(dve):
            dve.wait_ge(consts_in, 16 * 9)
            dve.wait_ge(pool_consts, 20 + 2 * GROUP)
            nc.vector.tensor_scalar(spread[:, 0, :], ones[:, 0:D], bq_c, None, ALU.mult).then_inc(spread_done, 1)
            nc.vector.tensor_scalar(spread[:, 1, :], ones[:, 0:D], a2_c, None, ALU.mult).then_inc(spread_done, 1)
            nc.vector.tensor_copy(wk_bk[:, 0:D], wk_sb).then_inc(spread_done, 1)
            nc.vector.tensor_copy(wk_bk[:, D:DE], bk_c).then_inc(spread_done, 1)
            nc.vector.tensor_copy(iota_row16[:, :], iota_row[:, :]).then_inc(dve_consts, 1)
            nc.vector.tensor_copy(ident16[:, :], ident[:, :]).then_inc(dve_consts, 1)
            for s in range(SEGS):
                nc.vector.tensor_scalar(shifted[:, s, :], ident[:, :], float(2 ** (s + PLACE_BITS)), None, ALU.mult)\
                  .then_inc(dve_consts, 1)
            dve.wait_ge(w_turned, 2)
            nc.vector.tensor_copy(wT[:, :, :], bank(0)[:, 0:2 * D].rearrange("p (n d) -> p n d", n=2))\
              .then_inc(w_turned_sb, 1)
            dve.wait_ge(mixed, 1)
            nc.vector.tensor_copy(mix[:, 0, D:DE], bank(1)[:, 0:1]).then_inc(mixed_sb, 1)
            nc.vector.tensor_copy(mix_bias[:, 0, 0:D], bank(1)[:, 128:256]).then_inc(mixed_sb, 1)
            nc.vector.tensor_copy(mix[:, 1, :], bank(2)[:, 0:DE]).then_inc(mixed_sb, 1)
            nc.vector.tensor_copy(mix_bias[:, 1, :], bank(3)[:, 0:DE]).then_inc(mixed_sb, 1)
            nc.vector.tensor_copy(mix_col[:, 0:1], bank(1)[:, 1:2]).then_inc(mixed_sb, 1)
            nc.vector.tensor_copy(mix_col[:, 1:2], bank(1)[:, 2:3]).then_inc(mixed_sb, 1)
            nc.vector.tensor_copy(obias[:, 1, :], bank(1)[:, 256:384]).then_inc(mixed_sb, 1)
            nc.vector.tensor_copy(proj[:, 0, :], w_sb).then_inc(mixed_sb, 1)
            nc.vector.tensor_copy(proj[:, 1, :], wT[:, 1, :]).then_inc(mixed_sb, 1)

            def moments(nth):
                with dve.Fori(0, T) as i:
                    nc.vector.bn_stats(stats[:, bass.ds(i, 1), :], X[:, bass.ds(i, 1), :]).then_inc(stats_done, 1)
                dve.wait_ge(stats_done, nth * T)
                nc.vector.tensor_tensor(half_gap[:, :], stats[:, :, 1], stats[:, :, 4], ALU.subtract).then_inc(gap_done, 1)
                nc.vector.tensor_tensor(mean[:, :], stats[:, :, 1], stats[:, :, 4], ALU.add).then_inc(mean_done, 1)
                nc.vector.tensor_tensor(var[:, :], stats[:, :, 2], stats[:, :, 5], ALU.add).then_inc(var_done, 1)
                dve.wait_ge(gap_done, 3 * nth - 2)
                nc.vector.tensor_tensor(half_gap[:, :], half_gap[:, :], half_gap[:, :], ALU.mult).then_inc(gap_done, 1)
                dve.wait_ge(gap_done, 3 * nth - 1)
                nc.vector.tensor_scalar(half_gap[:, :], half_gap[:, :], 0.25, None, ALU.mult).then_inc(gap_done, 1)
                dve.wait_ge(gap_done, 3 * nth)
                dve.wait_ge(var_done, 2 * nth - 1)
                nc.vector.scalar_tensor_tensor(out=var[:, :], in0=var[:, :], scalar=1.0 / D, in1=half_gap[:, :],
                                               op0=ALU.mult, op1=ALU.add).then_inc(var_done, 1)
                dve.wait_ge(sd_done, nth)
                nc.vector.reciprocal(rstd[:, :], sd[:, :]).then_inc(rstd_done, 1)
                dve.wait_ge(rstd_done, nth)
                dve.wait_ge(mean_done, nth)
                nc.vector.scalar_tensor_tensor(out=shift[:, :], in0=mean[:, :], scalar=-0.5, in1=rstd[:, :],
                                               op0=ALU.mult, op1=ALU.mult).then_inc(shift_done, 1)

            def keep_u(layer):
                def pair(j, first, last):
                    for k in range(2):
                        g = 2 * j + k
                        dve.wait_ge(h_turned, g + 1 + layer * G)
                        nc.vector.tensor_copy(stageT[:, k, :], bank(k)[:, :]).then_inc(ht_done, 1)
                        if not (first and k == 0):
                            leave(g - 1, (k + 1) % 2)
                    if last:
                        leave(g, k)

                def leave(g, k):
                    dve.wait_ge(u_done, g + 1 + layer * G)
                    for n in range(2):
                        t = g * GROUP + 2 * n
                        nc.vector.tensor_tensor(U[:, bass.ds(t, 2), :],
                                                bank(2 + 2 * k + n)[:, :].rearrange("p (a d) -> p a d", a=2)[:, :, 0:DE],
                                                mix_bias[:, layer:layer + 1, :].to_broadcast([P, 2, DE]), ALU.add)\
                          .then_inc(u_kept, 1)

                in_pairs(dve, pair)

            dve.wait_ge(x_in, 16)
            moments(1)
            keep_u(0)

            def extract(g, b):
                t = g * GROUP + b
                v = V[b % 2]
                dve.wait_ge(packed, t + 1)
                dve.sem_inc(sel_ready, 1)
                nc.vector.max(words[:, b, 0:8], v).then_inc(top_done, 1)
                dve.wait_ge(top_done, 3 * t + 1)
                dve.sem_inc(sel_ready, 1)
                nc.vector.match_replace(rest[:, 0, :], words[:, b, 0:8], v, 0.0).then_inc(rest_done, 1)
                dve.wait_ge(rest_done, 2 * t + 1)
                dve.sem_inc(sel_ready, 1)
                nc.vector.max(words[:, b, 8:16], rest[:, 0, :]).then_inc(top_done, 1)
                dve.wait_ge(top_done, 3 * t + 2)
                dve.sem_inc(sel_ready, 1)
                nc.vector.match_replace(rest[:, 1, :], words[:, b, 8:16], rest[:, 0, :], 0.0).then_inc(rest_done, 1)
                dve.wait_ge(rest_done, 2 * t + 2)
                dve.sem_inc(sel_ready, 1)
                nc.vector.max(words[:, b, 16:24], rest[:, 1, :]).then_inc(top_done, 1)

            flat = words.rearrange("p b k -> p (b k)")
            DECODE = 13

            def decode(g):
                step = [0]

                def done(ins):
                    ins.then_inc(decoded, 1)
                    step[0] += 1

                def after(n=None):
                    dve.wait_ge(decoded, DECODE * g + (step[0] if n is None else n))

                dve.wait_ge(top_done, 3 * GROUP * (g + 1))
                done(nc.vector.tensor_copy(words_i[:, :], flat))
                nc.vector.tensor_copy(widest_all[:, bass.ds(g * GROUP, GROUP)], words[:, :, 0]).then_inc(lists_done, 1)
                after()
                done(nc.vector.tensor_single_scalar(place_i[:, :], words_i[:, :], 2 ** PLACE_BITS - 1, ALU.bitwise_and))
                done(nc.vector.tensor_single_scalar(bits_i[:, :], words_i[:, :], PLACE_BITS, ALU.arith_shift_right))
                after(3)
                done(nc.vector.tensor_scalar(place_f[:, :], place_i[:, :], float(1 - 127 * BLOCK), None, ALU.add))
                done(nc.vector.tensor_copy(bits_f[:, 0, :], bits_i[:, :]))
                for n in range(DEPTH):
                    after()
                    done(nc.vector.tensor_single_scalar(top_f[:, n, :].bitcast(I32), bits_f[:, n, :].bitcast(I32),
                                                        0x7F800000, ALU.bitwise_and))
                    if n + 1 < DEPTH:
                        after()
                        done(nc.vector.tensor_tensor(bits_f[:, n + 1, :], bits_f[:, n, :], top_f[:, n, :], ALU.subtract))
                after()
                done(nc.vector.tensor_single_scalar(expo_i[:, :, :], top_f[:, :, :].bitcast(I32), 23,
                                                    ALU.arith_shift_right))
                after()
                done(nc.vector.scalar_tensor_tensor(
                    out=node_f[:, :, :], in0=expo_i[:, :, :], scalar=float(BLOCK),
                    in1=place_f[:, :].rearrange("p (o k) -> p o k", o=1).to_broadcast([P, DEPTH, GROUP * WORDS]),
                    op0=ALU.mult, op1=ALU.add))
                after()
                done(nc.vector.scalar_tensor_tensor(
                    out=found.rearrange("p n b k -> p (n b k)"), in0=top_f.rearrange("p n k -> p (n k)"), scalar=0.0,
                    in1=node_f.rearrange("p n k -> p (n k)"), op0=ALU.is_gt, op1=ALU.mult))
                assert step[0] == DECODE, step
                after()
                for b in range(GROUP):
                    t = g * GROUP + b
                    now, k = found[:, :, b, :], 0
                    while True:
                        dve.sem_inc(sel_ready, 1)
                        nc.vector.max(listed[:, b, 8 * k:8 * k + 8], now).then_inc(ltop_done, 1)
                        k += 1
                        if 8 * k == SLOTS:
                            break
                        dve.wait_ge(ltop_done, (SLOTS // 8) * t + k)
                        dve.sem_inc(sel_ready, 1)
                        nxt = found2[:, (k - 1) % 2, :].rearrange("p (n k) -> p n k", n=DEPTH)
                        nc.vector.match_replace(nxt, listed[:, b, 8 * k - 8:8 * k], now, 0.0).then_inc(lrest_done, 1)
                        dve.wait_ge(lrest_done, (SLOTS // 8 - 1) * t + k)
                        now = nxt
                dve.wait_ge(ltop_done, (SLOTS // 8) * GROUP * (g + 1))
                nc.vector.tensor_scalar(is_listed[:, :, :], listed[:, :, 0:SLOTS], 0.0, None, ALU.is_gt).then_inc(count_done, 1)
                dve.wait_ge(count_done, 3 * g + 1)
                nc.vector.tensor_reduce(count4[:, :], is_listed[:, :, :], AX.X, ALU.add).then_inc(count_done, 1)
                dve.wait_ge(count_done, 3 * g + 2)
                nc.vector.tensor_copy(count_all[:, bass.ds(g * GROUP, GROUP)], count4[:, :]).then_inc(lists_done, 1)
                nc.vector.tensor_copy(count16[:, :], count4[:, :]).then_inc(count_done, 1)

            def split(g):
                dve.wait_ge(ends_done, g + 1)
                nc.vector.tensor_copy(end4[:, :], bank(6)[:, 0:GROUP]).then_inc(split_done, 1)
                dve.wait_ge(split_done, 6 * g + 1)
                nc.vector.tensor_copy(end_all[:, bass.ds(g * GROUP, GROUP)], end4[:, :]).then_inc(lists_done, 1)
                nc.vector.tensor_tensor(listed[:, :, SLOTS], end4[:, :], count4[:, :], ALU.subtract).then_inc(split_done, 1)
                dve.wait_ge(split_done, 6 * g + 2)
                nc.vector.tensor_copy(listed_i[:, :], listed.rearrange("p b k -> p (b k)")).then_inc(split_done, 1)
                dve.wait_ge(split_done, 6 * g + 3)
                nc.vector.tensor_single_scalar(lo_i[:, :], listed_i[:, :], 63, ALU.bitwise_and).then_inc(split_done, 1)
                dve.wait_ge(split_done, 6 * g + 4)
                low = lo_i.rearrange("p (b k) -> p b k", b=GROUP)
                nc.vector.tensor_copy(lo16[:, :, 0:SLOTS + 1], low).then_inc(split_done, 1)
                nc.vector.tensor_tensor(hi16[:, :, 0:SLOTS + 1], listed[:, :, :], low, ALU.subtract).then_inc(split_done, 1)

            def mark(g, b):
                t = g * GROUP + b
                nc.vector.tensor_scalar(from_pre[:, :], iota16[:, :], listed[:, b, SLOTS:SLOTS + 1], None, ALU.is_ge)\
                  .then_inc(mine_done, 1)
                nc.vector.tensor_scalar(from_end[:, :], iota16[:, :], end4[:, b:b + 1], None, ALU.is_ge)\
                  .then_inc(mine_done, 1)
                dve.wait_ge(mine_done, 3 * t + 2)
                nc.vector.tensor_tensor(mine[:, b % 2, :], from_pre[:, :], from_end[:, :], ALU.subtract)\
                  .then_inc(mine_done, 1)
                dve.wait_ge(mine_done, 3 * t + 3)

            def pick(g, b):
                t = g * GROUP + b
                ps = q_lists[b % 2]
                at = bass.ds(t, 1)
                wide = lambda v: v.to_broadcast([P, CHUNKS, SLOTS])
                dve.wait_ge(q_done, t + 1)
                nc.vector.tensor_tensor(slot_all[:, at, :], iota_q.rearrange("p (o c) -> p o c", o=1),
                                        ps[:, :, SLOTS].rearrange("p (o c) -> p o c", o=1), ALU.subtract)\
                  .then_inc(pick_done, 1)
                nc.vector.tensor_copy(owner_all[:, at, :], ps[:, :, SLOTS + 1].rearrange("p (o c) -> p o c", o=1))\
                  .then_inc(lists_done, 1)
                dve.wait_ge(pick_done, 6 * t + 1)
                nc.vector.tensor_tensor(one_hot[:, :, :], wide(iota_slot.rearrange("p (o k) -> p o k", o=1)),
                                        wide(slot_all[:, at, :].rearrange("p o c -> p c o")), ALU.is_equal)\
                  .then_inc(pick_done, 1)
                dve.wait_ge(pick_done, 6 * t + 2)
                nc.vector.tensor_tensor(picked[:, :, :], ps[:, :, 0:SLOTS], one_hot[:, :, :], ALU.mult).then_inc(pick_done, 1)
                dve.wait_ge(pick_done, 6 * t + 3)
                nc.vector.tensor_reduce(node_q[:, :], picked[:, :, :], AX.X, ALU.add).then_inc(pick_done, 1)
                dve.wait_ge(pick_done, 6 * t + 4)
                nc.vector.tensor_scalar(past_q[:, :], node_q[:, :], 0.0, float(2 * N), ALU.is_equal, ALU.mult)\
                  .then_inc(pick_done, 1)
                dve.wait_ge(pick_done, 6 * t + 5)
                nc.vector.scalar_tensor_tensor(out=idx_all[:, at, :], in0=node_q.rearrange("p (o c) -> p o c", o=1),
                                               scalar=-1.0, in1=past_q.rearrange("p (o c) -> p o c", o=1),
                                               op0=ALU.add, op1=ALU.add).then_inc(pick_done, 1)

            def survey_group(g, first, last):
                for b in range(GROUP):
                    extract(g, b)
                    if not first:
                        if b == 0:
                            split(g - 1)
                            dve.wait_ge(split_done, 6 * g)
                            mark(g - 1, 0)
                        else:
                            pick(g - 1, b - 1)
                        if b + 1 < GROUP:
                            mark(g - 1, b + 1)
                if not first:
                    pick(g - 1, GROUP - 1)
                decode(g)
                if last:
                    split(g)
                    dve.wait_ge(split_done, 6 * (g + 1))
                    for b in range(GROUP):
                        mark(g, b)
                        if b:
                            pick(g, b - 1)
                    pick(g, GROUP - 1)

            groups(dve, survey_group)

            dve.wait_ge(lists_done, 3 * G + T)
            dve.wait_ge(mask_done, QUARTERS * T)
            nc.vector.tensor_reduce(half_gap[:, :], sum_all[:, :, :], AX.X, ALU.add).then_inc(bad_done, 1)
            dve.wait_ge(bad_done, 1)
            nc.vector.tensor_tensor(half_gap[:, :], half_gap[:, :], count_all[:, :], ALU.not_equal).then_inc(bad_done, 1)
            dve.wait_ge(bad_done, 2)
            nc.vector.tensor_reduce(bad[:, 0:1], half_gap[:, :], AX.X, ALU.max).then_inc(bad_done, 1)
            nc.vector.tensor_scalar(var[:, :], widest_all[:, :], float(EXACT) - 1.0, None, ALU.is_gt).then_inc(bad_done, 1)
            dve.wait_ge(bad_done, 4)
            nc.vector.tensor_reduce(bad[:, 1:2], var[:, :], AX.X, ALU.max).then_inc(bad_done, 1)
            nc.vector.tensor_scalar(sd[:, :], end_all[:, :], float(QCOLS), None, ALU.is_gt).then_inc(bad_done, 1)
            dve.wait_ge(bad_done, 6)
            nc.vector.tensor_reduce(bad[:, 2:3], sd[:, :], AX.X, ALU.max).then_inc(bad_done, 1)
            nc.vector.tensor_scalar(mean[:, :], count_all[:, :], 1.0, None, ALU.is_lt).then_inc(bad_done, 1)
            dve.wait_ge(bad_done, 8)
            nc.vector.tensor_reduce(bad[:, 3:4], mean[:, :], AX.X, ALU.max).then_inc(bad_done, 1)
            dve.wait_ge(bad_done, 9)
            nc.vector.tensor_reduce(bad_row[:, :], bad[:, :], AX.X, ALU.max).then_inc(bad_done, 1)
            dve.wait_ge(bad_summed, 1)
            nc.vector.tensor_scalar(flag[0:1, :], bank(7)[0:1, 0:1], 0.5, None, ALU.is_gt).then_inc(flag_done, 1)
            dve.wait_ge(flag_done, 1)
            whole = dve.value_load(flag[0:1, 0:1], min_val=0, max_val=1)

            with dve.If(whole > 0):
                for layer in range(2):
                    base = layer * T
                    if layer:
                        dve.wait_ge(w_x_done, T)
                        moments(2)
                    with dve.Fori(0, WCHUNKS) as i:
                        dve.wait_ge(w_h_turned, i + 1 + layer * WCHUNKS)
                        nc.vector.tensor_copy(wHT[:, bass.ds(i * WCH, WCH)], wpsT[0]).then_inc(w_ht_done, 1)

                    with dve.Fori(0, T) as i:
                        t = i + base
                        dve.wait_ge(w_u_done, t + 1)
                        nc.vector.tensor_scalar(wcbias[:, :], bank(7)[:, 0:1], mix_bias[:, layer, D:DE],
                                                1.0 if layer == 0 else SCALE, ALU.add, ALU.mult).then_inc(w_cbias_done, 1)
                        for q in range(QUARTERS):
                            piece = wS[:, q * QUARTER:(q + 1) * QUARTER]
                            dve.wait_ge(w_s_moved, WCHUNKS * t + -(-(q + 1) * QUARTER // WCH))
                            if layer == 0:
                                nc.vector.scalar_tensor_tensor(out=piece, in0=piece, scalar=ALPHA, in1=piece,
                                                               op0=ALU.mult, op1=ALU.max).then_inc(w_leaky_done, 1)
                            if q:
                                dve.wait_ge(w_masked, QUARTERS * t + q)
                            dve.wait_ge(w_adj_in[q], 16 * t + 16)
                            nc.vector.tensor_scalar(penalty[:, :], wadj[:, q, :], 0.0, NEG, ALU.is_le, ALU.mult)\
                              .then_inc(w_penalty_done, 1)
                            if layer == 0:
                                dve.wait_ge(w_leaky_done, QUARTERS * t + q + 1)
                            dve.wait_ge(w_penalty_done, QUARTERS * t + q + 1)
                            dve.sem_inc(w_adj_used[q], 1)
                            nc.vector.tensor_tensor_reduce(out=piece, in0=piece, in1=penalty[:, :], scale=1.0,
                                                           scalar=-3.0e38, op0=ALU.add, op1=ALU.max,
                                                           accum_out=wpmax[:, q:q + 1]).then_inc(w_masked, 1)
                        dve.wait_ge(w_masked, QUARTERS * t + QUARTERS)
                        nc.vector.tensor_reduce(wnmax[:, :], wpmax[:, :], AX.X, ALU.max).then_inc(w_pmax_done, 1)
                        dve.wait_ge(w_pmax_done, t + 1)
                        nc.vector.tensor_scalar(wnmax[:, :], wnmax[:, :], -1.0, None, ALU.mult).then_inc(w_nmax_done, 1)
                        dve.wait_ge(w_exp_done, t + 1)
                        nc.vector.reciprocal(wrrec[:, :], wrsum[:, :]).then_inc(w_rrec_done, 1)
                        dve.wait_ge(w_a_done, t + 1)
                        nc.vector.tensor_copy(wAT[:, :], bank(4)[:, 0:P]).then_inc(w_at_done, 1)
                        dve.wait_ge(w_rrec_done, t + 1)
                        dve.wait_ge(w_o_done, t + 1)
                        nc.vector.scalar_tensor_tensor(out=wz[:, :], in0=bank(5)[:, 0:D], scalar=wrrec[:, 0:1],
                                                       in1=obias[:, layer, :], op0=ALU.mult, op1=ALU.add).then_inc(w_z_done, 1)
                        dve.wait_ge(w_z_done, t + 1)
                        nc.vector.tensor_scalar(wzneg[:, :], wz[:, :], 0.0, None, ALU.min).then_inc(w_zneg_done, 1)
                        nc.vector.tensor_scalar(wzpos[:, :], wz[:, :], 0.0, -1.0, ALU.max, ALU.add).then_inc(w_zpos_done, 1)
                        dve.wait_ge(w_zexp_done, t + 1)
                        dve.wait_ge(w_zpos_done, t + 1)
                        nc.vector.tensor_tensor(wzpos[:, :], wzpos[:, :], wzexp[:, :], ALU.add).then_inc(w_y_done, 1)
                        dve.wait_ge(w_y_done, t + 1)
                        nc.vector.tensor_tensor(X[:, bass.ds(i, 1), :], X[:, bass.ds(i, 1), :],
                                                wzpos.rearrange("p (o d) -> p o d", o=1), ALU.add).then_inc(w_x_done, 1)
            with dve.Else():
                for layer in range(2):
                    base = layer * T
                    if layer:
                        dve.wait_ge(x_done, T)
                        moments(2)
                        keep_u(1)
                    wide_p = lambda v: v.to_broadcast([P, CHUNKS, P])
                    wide_k = lambda v: v.to_broadcast([P, CHUNKS, SLOTS])
                    cut = lambda v: v.rearrange("p (c o) -> p c o", o=1)

                    def own(t, b):
                        for c in range(CHUNKS):
                            last_one = nc.vector.tensor_scalar(
                                owned[:, b % GROUP, c, :], iota_row16[:, :],
                                owner_all[:, bass.ds(t, 1), c:c + 1].rearrange("p o c -> p (o c)"), None, ALU.is_equal)
                        last_one.then_inc(owned_done, 1)

                    def hot(t, b):
                        nc.vector.tensor_tensor(slot_hot[:, b % GROUP, :, :], wide_k(iota_slot.rearrange("p (o k) -> p o k", o=1)),
                                                wide_k(slot_all[:, bass.ds(t, 1), :].rearrange("p o c -> p c o")),
                                                ALU.is_equal).then_inc(hot_done, 1)

                    def products(g, b):
                        t = g * GROUP + b
                        tt = t + base
                        nc.vector.tensor_scalar(pad[:, :], iota_slot[:, :], count_all[:, bass.ds(t, 1)], NEG,
                                                ALU.is_ge, ALU.mult).then_inc(pad_done, 1)
                        dve.wait_ge(rows_in[b % GROUP], (g + b // GROUP + 1 + layer * G) * 16 * CHUNKS)
                        for u in range(4):
                            c0, c1 = 3 * u, min(3 * u + 3, CHUNKS)
                            dve.wait_ge(spread_u, 4 * tt + u + 1)
                            nc.vector.tensor_tensor(prod[:, c0:c1, :], bank(2 + u % 2)[:, 0:(c1 - c0) * DE]
                                                    .rearrange("p (c d) -> p c d", d=DE),
                                                    Gt[:, b % GROUP, c0:c1, :], ALU.mult).then_inc(prod_done, 1)

                    def scores(t, b):
                        tt = t + base
                        dve.wait_ge(prod_done, 4 * tt + 4)
                        nc.vector.tensor_reduce(raw[:, :], prod[:, :, :], AX.X, ALU.add).then_inc(raw_done, 1)
                        dve.wait_ge(raw_done, tt + 1)
                        for to in (score[:, b % 2, :], score16[:, 0, :]):
                            if layer == 0:
                                nc.vector.scalar_tensor_tensor(out=to, in0=raw[:, :], scalar=ALPHA, in1=raw[:, :],
                                                               op0=ALU.mult, op1=ALU.max).then_inc(score_done, 1)
                            else:
                                nc.vector.tensor_scalar(to, raw[:, :], SCALE, None, ALU.mult).then_inc(score_done, 1)
                        dve.wait_ge(score_done, 3 * tt + 2)
                        nc.vector.tensor_tensor(score16[:, 1, :], score[:, b % 2, :], score16[:, 0, :], ALU.subtract)\
                          .then_inc(score_done, 1)
                        dve.wait_ge(score_done, 3 * tt + 3)
                        dve.wait_ge(hot_done, tt + 1)
                        nc.vector.tensor_tensor(
                            slot_e[:, :, :, :],
                            slot_hot[:, b % GROUP:b % GROUP + 1, :, :].to_broadcast([P, 2, CHUNKS, SLOTS]),
                            score16.rearrange("p n (c o) -> p n c o", o=1).to_broadcast([P, 2, CHUNKS, SLOTS]),
                            ALU.mult).then_inc(slot_e_done, 1)

                    def maxima(t, b):
                        tt = t + base
                        dve.wait_ge(scattered, tt + 1)
                        dve.wait_ge(pad_done, tt + 1)
                        nc.vector.tensor_tensor(by_slot[:, :], bank(4)[:, 0:SLOTS], pad[:, :], ALU.add).then_inc(by_slot_done, 1)
                        dve.wait_ge(by_slot_done, tt + 1)
                        for to in (row_max[:, :], max16[:, 0:1]):
                            nc.vector.tensor_reduce(to, by_slot[:, :], AX.X, ALU.max).then_inc(max_done, 1)
                        dve.wait_ge(max_done, 3 * tt + 2)
                        nc.vector.tensor_tensor(max16[:, 1:2], row_max[:, :], max16[:, 0:1], ALU.subtract).then_inc(max_done, 1)

                    def below(t, b):
                        tt = t + base
                        dve.wait_ge(max_spread, tt + 1)
                        nc.vector.tensor_tensor(gap[:, :], score[:, b % 2, :], bank(5)[:, 0:CHUNKS], ALU.subtract).then_inc(below_done, 1)

                    def weigh(t, b):
                        tt = t + base
                        dve.wait_ge(prob_done, tt + 1)
                        nc.vector.tensor_tensor(weighted[:, b % 2, :, :], owned[:, b % GROUP, :, :], wide_p(cut(prob)), ALU.mult)\
                          .then_inc(weighted_done, 1)

                    def inverse(t, b):
                        dve.wait_ge(acc_done, t + base + 1)
                        nc.vector.reciprocal(rsum[:, :], bank(6)[:, D:DE]).then_inc(rsum_done, 1)

                    def finish(t, b):
                        tt = t + base
                        dve.wait_ge(o_done, tt + 1)
                        nc.vector.tensor_tensor(z[:, :], bank(7)[:, 0:D], obias[:, layer, :], ALU.add).then_inc(z_done, 1)
                        dve.wait_ge(z_done, tt + 1)
                        nc.vector.tensor_scalar(zneg[:, :], z[:, :], 0.0, None, ALU.min).then_inc(zneg_done, 1)

                    def finish2(t, b):
                        tt = t + base
                        dve.wait_ge(zexp_done, tt + 1)
                        nc.vector.scalar_tensor_tensor(out=y[:, :], in0=z[:, :], scalar=0.0, in1=zexp[:, :],
                                                       op0=ALU.max, op1=ALU.add).then_inc(y_done, 1)
                        dve.wait_ge(y_done, tt + 1)
                        at = bass.ds(t, 1)
                        nc.vector.scalar_tensor_tensor(out=X[:, at, :], in0=y.rearrange("p (o d) -> p o d", o=1), scalar=-1.0,
                                                       in1=X[:, at, :], op0=ALU.add, op1=ALU.add).then_inc(x_done, 1)

                    def attend_group(g, first, last):
                        if first:
                            for b in range(2):
                                own(b, b)
                                hot(b, b)
                            products(0, 0)
                            scores(0, 0)
                        for b in range(GROUP):
                            t = g * GROUP + b
                            before = not (first and b == 0)
                            after = not (last and b == GROUP - 1)
                            after2 = not (last and b >= GROUP - 2)
                            maxima(t, b)
                            if after:
                                products(g, b + 1)
                            below(t, b)
                            if before:
                                inverse(t - 1, b - 1)
                            if after:
                                scores(t + 1, b + 1)
                            if after2:
                                own(t + 2, b + 2)
                            weigh(t, b)
                            if after2:
                                hot(t + 2, b + 2)
                            if before:
                                finish(t - 1, b - 1)
                                finish2(t - 1, b - 1)
                        if last:
                            inverse(t, b)
                            finish(t, b)
                            finish2(t, b)

                    groups(dve, attend_group)

        @block.scalar
        def _(act):
            def sd_of(nth):
                act.wait_ge(var_done, 2 * nth)
                nc.scalar.activation(sd[:, :], var[:, :], ACT.Sqrt, bias=eps[:, 0:1]).then_inc(sd_done, 1)
                act.wait_ge(shift_done, nth)

            def rows_h(m, to, signal):
                nc.scalar.activation(to, X[:, bass.ds(m, 1), :], ACT.Relu, bias=shift[:, bass.ds(m, 1)],
                                     scale=rstd[:, bass.ds(m, 1)]).then_inc(signal, 1)

            def stage_h(layer):
                def pair(j, first, last):
                    for k in range(2):
                        g = 2 * j + k
                        if layer or not first:
                            act.wait_ge(table_written[k], 16 * j + 8 * G * layer)
                            act.wait_ge(h_turned, g - 1 + layer * G)
                        for b in range(GROUP):
                            rows_h(g * GROUP + b, stage[:, k, b:b + 1, :], h_done)

                in_pairs(act, pair)

            act.wait_ge(pool_consts, 20 + 2 * GROUP)
            sd_of(1)
            stage_h(0)

            def relu_tile(t, b, wait_packed):
                if wait_packed:
                    act.wait_ge(packed, t - 1)
                for q in range(QUARTERS):
                    act.wait_ge(adj_in[q], 16 * t + 16)
                    nc.scalar.activation(mask[:, b % 2, q * QUARTER:(q + 1) * QUARTER], adj_sb[:, q, :], ACT.Relu,
                                         accum_out=sum_all[:, bass.ds(t, 1), q:q + 1].rearrange("p o c -> p (o c)"))\
                      .then_inc(mask_done, 1)

            def relu_group(g, first, last):
                for b in range(GROUP):
                    relu_tile(g * GROUP + b, b, not (first and b < 2))

            groups(act, relu_group)

            act.wait_ge(flag_done, 1)
            whole = act.value_load(flag[0:1, 0:1], min_val=0, max_val=1)
            with act.If(whole > 0):
                for layer in range(2):
                    base = layer * T

                    def freed(i, layer=layer):
                        act.wait_ge(w_h_kept, i + layer * WCHUNKS)
                        act.wait_ge(w_h_turned, i + layer * WCHUNKS)

                    if layer:
                        sd_of(2)

                    def stage_group(g, first, last):
                        if layer or not first:
                            freed(g)
                        for b in range(GROUP):
                            rows_h(g * GROUP + b, wstage[:, b:b + 1, :], w_h_done)

                    groups(act, stage_group)
                    with act.Fori(0, T) as i:
                        t = i + base
                        act.wait_ge(w_u_done, t + 1)
                        nc.scalar.activation(wUT[:, :], bank(6)[:, 0:P], ACT.Identity, bias=mix_col[:, layer:layer + 1])\
                          .then_inc(w_ut_done, 1)
                        act.wait_ge(w_cbias_done, t + 1)
                        for c in range(WCHUNKS):
                            act.wait_ge(w_s_done, WCHUNKS * t + c + 1)
                            nc.scalar.activation(wS[:, c * WCH:(c + 1) * WCH], wpsS[c % 2], ACT.Identity,
                                                 bias=wcbias[:, 0:1], scale=1.0 if layer == 0 else SCALE).then_inc(w_s_moved, 1)
                        act.wait_ge(w_nmax_done, t + 1)
                        nc.scalar.activation(wS[:, :], wS[:, :], ACT.Exp, bias=wnmax[:, 0:1], accum_out=wrsum[:, 0:1])\
                          .then_inc(w_exp_done, 1)
                        for c in range(WCHUNKS):
                            act.wait_ge(w_p_turned, WCHUNKS * t + c + 1)
                            if c >= 2:
                                act.wait_ge(w_pt_used, WCHUNKS * t + c - 1)
                            nc.scalar.activation(wPT[:, c % 2, :], wpsT[c % 2], ACT.Identity).then_inc(w_pt_done, 1)
                        act.wait_ge(w_zneg_done, t + 1)
                        nc.scalar.activation(wzexp[:, :], wzneg[:, :], ACT.Exp).then_inc(w_zexp_done, 1)
            with act.Else():
                for layer in range(2):
                    base = layer * T
                    if layer:
                        sd_of(2)
                        stage_h(1)

                    def move_owners(t, b):
                        for u in range(2):
                            half = slice(u * CHUNKS // 2, (u + 1) * CHUNKS // 2)
                            act.wait_ge(turned, 2 * (t + base) + u + 1)
                            for to in (owners, owners16):
                                last_one = nc.scalar.activation(to[:, b % GROUP, half, :].rearrange("p c q -> p (c q)"),
                                                                turned_ps[u], ACT.Identity)
                            last_one.then_inc(owners_done, 1)

                    def move_acc(t, b):
                        tt = t + base
                        act.wait_ge(rsum_done, tt + 1)
                        nc.scalar.activation(acc[:, :], bank(6)[:, 0:P], ACT.Identity, scale=rsum[:, 0:1]).then_inc(acc_sb, 1)
                        act.wait_ge(acc_turned, tt + 1)
                        nc.scalar.activation(accT[:, :], bank(7)[:, 0:P], ACT.Identity).then_inc(accT_sb, 1)

                    def exp_z(t, b):
                        act.wait_ge(zneg_done, t + base + 1)
                        nc.scalar.activation(zexp[:, :], zneg[:, :], ACT.Exp).then_inc(zexp_done, 1)

                    def attend_group(g, first, last):
                        if first:
                            move_owners(0, 0)
                            move_owners(1, 1)
                        for b in range(GROUP):
                            t = g * GROUP + b
                            before = not (first and b == 0)
                            act.wait_ge(below_done, t + base + 1)
                            nc.scalar.activation(prob[:, :], gap[:, :], ACT.Exp).then_inc(prob_done, 1)
                            if before:
                                move_acc(t - 1, b - 1)
                            if not (last and b >= GROUP - 2):
                                move_owners(t + 2, b + 2)
                            if before:
                                exp_z(t - 1, b - 1)
                        if last:
                            move_acc(t, b)
                            exp_z(t, b)

                    groups(act, attend_group)

        @block.tensor
        def _(pe):
            pe.wait_ge(consts_in, 16 * 9)
            pe.wait_ge(pool_consts, 20 + 2 * GROUP)
            nc.tensor.transpose(bank(0)[:, 0:D], w_sb, ident[:, :]).then_inc(w_turned, 1)
            nc.tensor.transpose(bank(0)[:, D:2 * D], wv_sb, ident[:, :]).then_inc(w_turned, 1)
            pe.wait_ge(w_turned_sb, 1)
            pe.wait_ge(spread_done, 4)
            nc.tensor.matmul(bank(1)[:, 0:1], wT[:, 0, :], a1_c, start=True, stop=True)
            nc.tensor.matmul(bank(1)[:, 1:2], wT[:, 0, :], a2_c, start=True, stop=True)
            nc.tensor.matmul(bank(1)[:, 2:3], wk_sb, bq_c, start=True, stop=True)
            nc.tensor.matmul(bank(1)[:, 128:256], spread[:, 1, :], wT[:, 0, :], start=True, stop=True)
            nc.tensor.matmul(bank(1)[:, 256:384], ones[0:1, 0:P], bvrow[0:1, :], start=True, stop=True)
            nc.tensor.matmul(bank(2)[:, 0:DE], wq_sb, wk_bk[:, :], start=True, stop=True)
            nc.tensor.matmul(bank(3)[:, 0:DE], spread[:, 0, :], wk_bk[:, :], start=True, stop=True).then_inc(mixed, 1)
            pe.wait_ge(mixed_sb, 9)

            def make_u(layer):
                def pair(j, first, last):
                    for k in range(2):
                        g = 2 * j + k
                        pe.wait_ge(h_done, (g + 1) * GROUP + layer * T)
                        if layer or not first:
                            pe.wait_ge(ht_done, g - 1 + layer * G)
                        for b in range(GROUP):
                            last_one = nc.tensor.transpose(bank(k)[:, b * P:(b + 1) * P], stage[:, k, b, :], ident[:, :])
                        last_one.then_inc(h_turned, 1)
                        if not (first and k == 0):
                            make(g - 1, (k + 1) % 2, first and k < 2)
                    if last:
                        make(g, k, False)

                def make(g, k, early):
                    pe.wait_ge(ht_done, g + 1 + layer * G)
                    if layer or not early:
                        pe.wait_ge(u_kept, 2 * (g - 1 + layer * G))
                    for b in range(GROUP):
                        last_one = nc.tensor.matmul(bank(2 + 2 * k + b // 2)[:, (b % 2) * 256:(b % 2) * 256 + DE],
                                                    stageT[:, k, b * P:(b + 1) * P], mix[:, layer, :], start=True, stop=True)
                    last_one.then_inc(u_done, 1)

                in_pairs(pe, pair)

            make_u(0)

            pe.wait_ge(dve_consts, SEGS + 2)
            pe.wait_ge(u_kept, 2 * G)

            def pack(g, b, wait_used):
                t = g * GROUP + b
                if wait_used:
                    pe.wait_ge(rest_done, 2 * t - 3)
                pe.wait_ge(mask_done, QUARTERS * (t + 1))
                for s in range(SEGS):
                    for c0, c1 in parts:
                        nc.tensor.matmul(V[b % 2][:, c0:c1], shifted[:, s, :],
                                         mask[:, b % 2, s * BLOCK + c0:s * BLOCK + c1], start=(s == 0), stop=False)
                for n, low in enumerate((place_hi, place_lo)):
                    for c0, c1 in parts:
                        last = nc.tensor.matmul(V[b % 2][:, c0:c1], ones16[0:1, :], low[0:1, c0:c1],
                                                start=False, stop=(n == 1))
                last.then_inc(packed, 1)

            def ends(g):
                pe.wait_ge(count_done, 3 * g + 3)
                nc.tensor.matmul(bank(6)[:, 0:GROUP], upto[:, :], count16[:, :], start=True, stop=True).then_inc(ends_done, 1)

            def deal(g, b):
                t = g * GROUP + b
                if b == 0:
                    pe.wait_ge(split_done, 6 * (g + 1))
                pe.wait_ge(mine_done, 3 * t + 3)
                for c in range(CHUNKS):
                    for part in (hi16, lo16):
                        last = nc.tensor.matmul(q_lists[b % 2][:, c, :], mine[:, b % 2, c * P:(c + 1) * P], part[:, b, :],
                                                start=(part is hi16), stop=(part is lo16))
                last.then_inc(q_done, 1)

            def survey_group(g, first, last):
                for b in range(GROUP):
                    pack(g, b, not (first and b < 2))
                    if not first:
                        if b == 0:
                            ends(g - 1)
                        else:
                            deal(g - 1, b - 1)
                if not first:
                    deal(g - 1, GROUP - 1)
                if last:
                    ends(g)
                    for b in range(GROUP):
                        deal(g, b)

            groups(pe, survey_group)
            pe.wait_ge(bad_done, 10)
            nc.tensor.matmul(bank(7)[:, 0:1], ones[:, 0:P], bad_row[:, :], start=True, stop=True).then_inc(bad_summed, 1)

            pe.wait_ge(flag_done, 1)
            whole = pe.value_load(flag[0:1, 0:1], min_val=0, max_val=1)
            with pe.If(whole > 0):
                for layer in range(2):
                    base = layer * T
                    def turn_rows(i, first):
                        pe.wait_ge(w_h_done, (i + 1) * WTILES + base)
                        if layer or not first:
                            pe.wait_ge(w_ht_done, i + layer * WCHUNKS)
                        for n in range(WTILES):
                            last = nc.tensor.transpose(wpsT[0][:, n * P:(n + 1) * P], wstage[:, n, :], ident[:, :])
                        last.then_inc(w_h_turned, 1)

                    counted(pe, WCHUNKS, turn_rows)
                    pe.wait_ge(w_ht_done, (layer + 1) * WCHUNKS)
                    pe.wait_ge(w_h_kept, (layer + 1) * WCHUNKS)
                    with pe.Fori(0, T) as i:
                        t = i + base
                        pe.wait_ge(w_rows_done, t + 1)
                        nc.tensor.matmul(bank(6)[:, 0:P], mix[:, layer, 0:D], wrows[:, :], start=True, stop=True)
                        nc.tensor.matmul(bank(7)[:, 0:1], wrows[:, :], mix[:, layer, D:DE], start=True, stop=True)\
                          .then_inc(w_u_done, 1)
                        pe.wait_ge(w_ut_done, t + 1)
                        for c in range(WCHUNKS):
                            if c >= 2:
                                pe.wait_ge(w_s_moved, WCHUNKS * t + c - 1)
                            nc.tensor.matmul(wpsS[c % 2], wUT[:, :], wHT[:, c * WCH:(c + 1) * WCH], start=True, stop=True)\
                              .then_inc(w_s_done, 1)
                        pe.wait_ge(w_exp_done, t + 1)

                        def weigh(c):
                            pe.wait_ge(w_pt_done, WCHUNKS * t + c + 1)
                            for n in range(WTILES):
                                last = nc.tensor.matmul(bank(4)[:, 0:P], wH[:, c * WTILES + n, :],
                                                        wPT[:, c % 2, n * P:(n + 1) * P], start=(c == 0 and n == 0),
                                                        stop=(c == WCHUNKS - 1 and n == WTILES - 1))
                            last.then_inc(w_pt_used, 1)

                        for c in range(WCHUNKS):
                            if c >= 2:
                                pe.wait_ge(w_pt_done, WCHUNKS * t + c - 1)
                            for n in range(WTILES):
                                at = c * WCH + n * P
                                last = nc.tensor.transpose(wpsT[c % 2][:, n * P:(n + 1) * P], wS[:, at:at + P], ident[:, :])
                            last.then_inc(w_p_turned, 1)
                            if c >= 1:
                                weigh(c - 1)
                        weigh(WCHUNKS - 1)
                        pe.wait_ge(w_pt_used, WCHUNKS * t + WCHUNKS)
                        pe.sem_inc(w_a_done, 1)
                        pe.wait_ge(w_at_done, t + 1)
                        nc.tensor.matmul(bank(5)[:, 0:D], wAT[:, :], proj[:, layer, :], start=True, stop=True)\
                          .then_inc(w_o_done, 1)
            with pe.Else():
                for layer in range(2):
                    base = layer * T
                    if layer:
                        make_u(1)
                    pe.wait_ge(u_kept, 2 * G * (layer + 1))

                    def turn(t, b):
                        tt = t + base
                        pe.wait_ge(owned_done, tt + 1)
                        for u in range(2):
                            if not (layer == 0 and isinstance(t, int) and t == 0):
                                pe.wait_ge(owners_done, 2 * tt + u - 1)
                            for n in range(CHUNKS // 2):
                                last = nc.tensor.transpose(turned_ps[u][:, n * P:(n + 1) * P],
                                                           owned[:, b % GROUP, u * CHUNKS // 2 + n, :], ident16[:, :])
                            last.then_inc(turned, 1)

                    def spread_rows(t, b, skip, which):
                        tt = t + base
                        if which[0] == 0:
                            pe.wait_ge(owners_done, 2 * tt + 2)
                        for u in which:
                            if not (skip and u < 2):
                                pe.wait_ge(prod_done, 4 * tt + u - 1)
                            for c in range(3 * u, min(3 * u + 3, CHUNKS)):
                                last = nc.tensor.matmul(bank(2 + u % 2)[:, (c % 3) * DE:(c % 3 + 1) * DE],
                                                        owners[:, b % GROUP, c, :],
                                                        U[:, bass.ds(t, 1), :].rearrange("p o d -> p (o d)"),
                                                        start=True, stop=True)
                            last.then_inc(spread_u, 1)

                    def turn_acc(t, b):
                        tt = t + base
                        pe.wait_ge(acc_sb, tt + 1)
                        pe.wait_ge(z_done, tt)
                        nc.tensor.transpose(bank(7)[:, 0:P], acc[:, :], ident[:, :]).then_inc(acc_turned, 1)

                    def project(t, b):
                        tt = t + base
                        pe.wait_ge(accT_sb, tt + 1)
                        nc.tensor.matmul(bank(7)[:, 0:D], accT[:, :], proj[:, layer, :], start=True, stop=True)\
                          .then_inc(o_done, 1)

                    def scatter(t, b):
                        pe.wait_ge(slot_e_done, t + base + 1)
                        for c in range(CHUNKS):
                            for n in range(2):
                                last = nc.tensor.matmul(bank(4)[:, 0:SLOTS], owned[:, b % GROUP, c, :], slot_e[:, n, c, :],
                                                        start=(c == 0 and n == 0), stop=(c == CHUNKS - 1 and n == 1))
                        last.then_inc(scattered, 1)

                    def spread_max(t, b):
                        pe.wait_ge(max_done, 3 * (t + base) + 3)
                        for c in range(CHUNKS):
                            for n in range(2):
                                last = nc.tensor.matmul(bank(5)[:, c:c + 1], owners16[:, b % GROUP, c, :], max16[:, n:n + 1],
                                                        start=(n == 0), stop=(n == 1))
                        last.then_inc(max_spread, 1)

                    def sum_up(t, b):
                        tt = t + base
                        pe.wait_ge(weighted_done, tt + 1)
                        pe.wait_ge(acc_sb, tt)
                        for c in range(CHUNKS):
                            last = nc.tensor.matmul(bank(6)[:, 0:DE], weighted[:, b % 2, c, :], Gt[:, b, c, :],
                                                    start=(c == 0), stop=(c == CHUNKS - 1))
                        last.then_inc(acc_done, 1)

                    def attend_group(g, first, last):
                        if first:
                            turn(0, 0)
                            turn(1, 1)
                            spread_rows(0, 0, layer == 0, (0, 1, 2, 3))
                            scatter(0, 0)
                        for b in range(GROUP):
                            t = g * GROUP + b
                            before = not (first and b == 0)
                            after = not (last and b == GROUP - 1)
                            if after:
                                spread_rows(t + 1, b + 1, False, (0, 1))
                            spread_max(t, b)
                            if after:
                                spread_rows(t + 1, b + 1, False, (2, 3))
                                scatter(t + 1, b + 1)
                            if before:
                                turn_acc(t - 1, b - 1)
                            if not (last and b >= GROUP - 2):
                                turn(t + 2, b + 2)
                            if before:
                                project(t - 1, b - 1)
                            sum_up(t, b)
                        if last:
                            turn_acc(t, b)
                            project(t, b)

                    groups(pe, attend_group)
_INS = ['x', 'adj', 'L0_gnn_W', 'L0_gnn_a', 'L1_gnn_Wq', 'L1_gnn_bq', 'L1_gnn_Wk', 'L1_gnn_bk', 'L1_gnn_Wv', 'L1_gnn_bv']
_OUTS = [((8192, 128), 'float32')]


def kernel(**inputs):
    import numpy as _np
    import concourse.bacc as _bacc
    from concourse import mybir as _mybir
    from concourse.bass_utils import run_bass_kernel_spmd as _run

    nc = _bacc.Bacc("TRN2", target_bir_lowering=False, num_devices=1)
    arrays, args = {}, []
    for name in _INS:
        a = _np.ascontiguousarray(inputs[name])
        arrays[f"in_{name}_dram"] = a
        args.append(nc.dram_tensor(f"in_{name}_dram", a.shape, _mybir.dt.from_np(a.dtype), kind="ExternalInput").ap())
    for i, (shape, dtype) in enumerate(_OUTS):
        dt = _mybir.dt.from_np(_np.dtype(dtype))
        args.append(nc.dram_tensor(f"out_{i}_dram", shape, dt, kind="ExternalOutput").ap())
    two_layer_graph_attention(nc, *args)
    r = _run(nc, [arrays], core_ids=[0])
    return r.results[0]["out_0_dram"]
```

```python
from contextlib import ExitStack

import concourse.bass as bass
from concourse import mybir

P = 128
F32 = mybir.dt.float32
F16 = mybir.dt.float16
BF16 = mybir.dt.bfloat16
I32 = mybir.dt.int32
U32 = mybir.dt.uint32
ALU = mybir.AluOpType
ACT = mybir.ActivationFunctionType
AX = mybir.AxisListType
NEG = -9000000000000000.0
ALPHA = 0.2
EPS = 1e-05

SEGS = 14
PLACE_BITS = 10
EXACT = 2 ** 24
WORDS = 24
DEPTH = 3
SLOTS = 24
CHUNKS = 10
GROUP = 4
QUARTERS = 4


def two_layer_graph_attention(nc, x, adj, W, a, Wq, bq, Wk, bk, Wv, bv, out):
    N, D = x.shape
    assert D == P and N % (2 * GROUP * P) == 0
    T = N // P
    G = T // GROUP
    SCALE = float(D) ** -0.5
    DE = D + 1
    QCOLS = CHUNKS * P
    BLOCK = -(-N // SEGS)
    QUARTER = N // QUARTERS
    assert BLOCK < 2 ** PLACE_BITS and SEGS + PLACE_BITS <= 24

    x_tiles = x.rearrange("(t p) d -> p t d", p=P)
    out_tiles = out.rearrange("(t p) d -> p t d", p=P)
    col = lambda v: v.rearrange("(p o) -> p o", o=1)
    tables = [nc.dram_tensor(f"table{n}", [N, D], F32, kind="Internal").ap() for n in range(2)]

    with ExitStack() as ctx:
        ARENA = 53000
        arena = ctx.enter_context(nc.sbuf_tensor("arena", [P, ARENA], F32))
        psum = ctx.enter_context(nc.psum_tensor("psum", [P, 8, 512], F32))
        sem = lambda name: ctx.enter_context(nc.semaphore(name))

        top = [0]

        def place(shape, dt=F32):
            count = 1
            for n in shape:
                count *= n
            words = -(-count * (2 if dt in (BF16, F16) else 4) // 4)
            words += words % 2
            v = arena[:, top[0]:top[0] + words]
            top[0] += words
            assert top[0] <= ARENA, top
            if dt != F32:
                v = v.bitcast(dt)
            v = v[:, 0:count]
            names = "abcd"[:len(shape)]
            if len(shape) > 1:
                v = v.rearrange(f"p ({' '.join(names)}) -> p {' '.join(names)}",
                                **{k: n for k, n in zip(names, shape)})
            return v

        X = place([T, D])
        ident = place([P])
        ones = place([DE])
        weights = place([4, D])
        w_sb, wq_sb, wk_sb, wv_sb = (weights[:, n, :] for n in range(4))
        wk_bk = place([DE])
        cols = place([4])
        a1_c, a2_c, bq_c, bk_c = (cols[:, n:n + 1] for n in range(4))
        bvrow = place([D])
        wT = place([2, D])
        spread = place([2, D])
        mix = place([2, DE])
        mix_bias = place([2, DE])
        mix_col = place([2])
        proj = place([2, D])
        obias = place([2, D])
        eps = place([1])
        stats = place([T, 6])
        half_gap = place([T])
        mean = place([T])
        var = place([T])
        sd = place([T])
        rstd = place([T])
        shift = place([T])
        bad = place([4])
        bad_row = place([1])
        flag = place([1], I32)
        common = top[0]

        U = place([T, DE])
        idx_all = place([T, CHUNKS], U32)
        owner_all = place([T, CHUNKS])
        slot_all = place([T, CHUNKS])
        count_all = place([T])
        sum_all = place([T, QUARTERS])
        end_all = place([T])
        widest_all = place([T])
        iota_q = place([CHUNKS])
        iota_slot = place([SLOTS])
        iota_row = place([P])
        iota_row16 = place([P], BF16)
        ident16 = place([P], BF16)
        lists = top[0]

        stage = place([2, GROUP, D])
        stageT = place([2, GROUP * P])
        adj_sb = place([QUARTERS, QUARTER], I32)
        mask = place([2, SEGS * BLOCK], BF16)
        shifted = place([SEGS, P], BF16)
        upto = place([P], BF16)
        ones16 = place([P], BF16)
        place_hi = place([BLOCK + 64], BF16)
        place_lo = place([BLOCK + 64], BF16)
        scratch = place([QCOLS], F32)
        iota16 = place([QCOLS], F16)
        rest = place([2, BLOCK])
        words = place([GROUP, WORDS])
        words_i = place([GROUP * WORDS], I32)
        place_i = place([GROUP * WORDS], I32)
        bits_i = place([GROUP * WORDS], I32)
        place_f = place([GROUP * WORDS])
        bits_f = place([DEPTH, GROUP * WORDS])
        top_f = place([DEPTH, GROUP * WORDS])
        expo_i = place([DEPTH, GROUP * WORDS], I32)
        node_f = place([DEPTH, GROUP * WORDS])
        found = place([DEPTH, GROUP, WORDS])
        found2 = place([2, DEPTH * WORDS])
        listed = place([GROUP, SLOTS + 1])
        is_listed = place([GROUP, SLOTS])
        count4 = place([GROUP])
        count16 = place([GROUP], BF16)
        end4 = place([GROUP])
        listed_i = place([GROUP * (SLOTS + 1)], I32)
        lo_i = place([GROUP * (SLOTS + 1)], I32)
        hi16 = place([GROUP, SLOTS + 2], BF16)
        lo16 = place([GROUP, SLOTS + 2], BF16)
        from_pre = place([QCOLS], BF16)
        from_end = place([QCOLS], BF16)
        mine = place([2, QCOLS], BF16)
        one_hot = place([CHUNKS, SLOTS])
        picked = place([CHUNKS, SLOTS])
        node_q = place([CHUNKS])
        past_q = place([CHUNKS])

        top[0] = lists
        top[0] += 4 * GROUP * P
        idx_now = place([GROUP, CHUNKS], U32)
        Gt = place([GROUP, CHUNKS, DE])
        owned = place([GROUP, CHUNKS, P], BF16)
        owners = place([GROUP, CHUNKS, P])
        owners16 = place([GROUP, CHUNKS, P], BF16)
        weighted = place([2, CHUNKS, P])
        slot_hot = place([GROUP, CHUNKS, SLOTS], BF16)
        slot_e = place([2, CHUNKS, SLOTS], BF16)
        score16 = place([2, CHUNKS], BF16)
        max16 = place([2], BF16)
        prod = place([CHUNKS, DE])
        raw = place([CHUNKS])
        score = place([2, CHUNKS])
        pad = place([SLOTS])
        by_slot = place([SLOTS])
        row_max = place([1])
        gap = place([CHUNKS])
        prob = place([CHUNKS])
        rsum = place([1])
        acc = place([P])
        accT = place([P])
        z = place([D])
        zneg = place([D])
        zexp = place([D])
        y = place([D])

        top[0] = common
        wH = place([T, D])
        wHT = place([N])
        wadj = place([QUARTERS, QUARTER], I32)
        wS = place([N])
        penalty = place([QUARTER])
        wPT = place([2, 512])
        wstage = place([GROUP, D])
        wrows = place([P])
        wUT = place([P])
        wcbias = place([1])
        wpmax = place([QUARTERS])
        wnmax = place([1])
        wrsum = place([1])
        wrrec = place([1])
        wAT = place([P])
        wz = place([D])
        wzneg = place([D])
        wzexp = place([D])
        wzpos = place([D])

        bank = lambda n: psum[:, n, :]
        parts = [(s, min(s + 512, BLOCK)) for s in range(0, BLOCK, 512)]
        V = [psum[:, 2 * v:2 * v + 2, :].rearrange("p a b -> p (a b)")[:, 0:BLOCK] for v in range(2)]
        q_lists = [bank(4 + v)[:, 0:CHUNKS * (SLOTS + 2)].rearrange("p (c k) -> p c k", c=CHUNKS) for v in range(2)]

        SPREADS = 4
        spread_parts = [(3 * u, min(3 * u + 3, CHUNKS)) for u in range(SPREADS)]
        assert spread_parts[-1][1] - spread_parts[-1][0] == 1 and spread_parts[-1][1] == CHUNKS
        spread_ps = [bank(n)[:, 0:3 * DE].rearrange("p (c d) -> p c d", d=DE) for n in (2, 3, 5)]
        by_slot_ps = bank(4)[:, 0:SLOTS]
        max_ps = bank(4)[:, 64:64 + CHUNKS]
        spread_ps.append(bank(4)[:, 128:128 + DE].rearrange("p (c d) -> p c d", d=DE))
        turned_ps = [bank(u)[:, 0:CHUNKS // 2 * P // 2].bitcast(BF16) for u in range(2)]

        consts_in = sem("consts_in")
        x_in = sem("x_in")
        pool_consts = sem("pool_consts")
        dve_consts = sem("dve_consts")
        spread_done = sem("spread_done")
        w_turned = sem("w_turned")
        w_turned_sb = sem("w_turned_sb")
        mixed = sem("mixed")
        mixed_sb = sem("mixed_sb")
        stats_done = sem("stats_done")
        gap_done = sem("gap_done")
        mean_done = sem("mean_done")
        var_done = sem("var_done")
        sd_done = sem("sd_done")
        rstd_done = sem("rstd_done")
        shift_done = sem("shift_done")
        h_done = sem("h_done")
        h_turned = sem("h_turned")
        ht_done = sem("ht_done")
        u_done = sem("u_done")
        u_kept = sem("u_kept")
        table_written = [sem(f"table_written{k}") for k in range(2)]
        adj_in = [sem(f"adj_in{q}") for q in range(QUARTERS)]
        mask_done = sem("mask_done")
        packed = sem("packed")
        top_done = sem("top_done")
        rest_done = sem("rest_done")
        decoded = sem("decoded")
        ltop_done = sem("ltop_done")
        lrest_done = sem("lrest_done")
        count_done = sem("count_done")
        ends_done = sem("ends_done")
        split_done = sem("split_done")
        in_step = sem("in_step")
        mine_done = sem("mine_done")
        q_done = sem("q_done")
        pick_done = sem("pick_done")
        lists_done = sem("lists_done")
        bad_done = sem("bad_done")
        bad_summed = sem("bad_summed")
        flag_done = sem("flag_done")
        idx_done = sem("idx_done")
        gathering = sem("gathering")
        rows_in = [sem(f"rows_in{b}") for b in range(GROUP)]
        owned_done = sem("owned_done")
        hot_done = sem("hot_done")
        turned = sem("turned")
        owners_done = sem("owners_done")
        spread_u = sem("spread_u")
        prod_done = sem("prod_done")
        raw_done = sem("raw_done")
        score_done = sem("score_done")
        slot_e_done = sem("slot_e_done")
        pad_done = sem("pad_done")
        scattered = sem("scattered")
        by_slot_done = sem("by_slot_done")
        max_done = sem("max_done")
        max_spread = sem("max_spread")
        below_done = sem("below_done")
        prob_done = sem("prob_done")
        weighted_done = sem("weighted_done")
        acc_done = sem("acc_done")
        rsum_done = sem("rsum_done")
        acc_sb = sem("acc_sb")
        acc_turned = sem("acc_turned")
        accT_sb = sem("accT_sb")
        o_done = sem("o_done")
        z_done = sem("z_done")
        zneg_done = sem("zneg_done")
        zexp_done = sem("zexp_done")
        y_done = sem("y_done")
        x_done = sem("x_done")
        out_written = sem("out_written")
        w_h_done = sem("w_h_done")
        w_h_kept = sem("w_h_kept")
        w_rows_done = sem("w_rows_done")
        w_h_turned = sem("w_h_turned")
        w_ht_done = sem("w_ht_done")
        w_adj_in = [sem(f"w_adj_in{q}") for q in range(QUARTERS)]
        w_adj_used = [sem(f"w_adj_used{q}") for q in range(QUARTERS)]
        w_u_done = sem("w_u_done")
        w_ut_done = sem("w_ut_done")
        w_cbias_done = sem("w_cbias_done")
        w_s_done = sem("w_s_done")
        w_s_moved = sem("w_s_moved")
        w_penalty_done = sem("w_penalty_done")
        w_leaky_done = sem("w_leaky_done")
        w_masked = sem("w_masked")
        w_pmax_done = sem("w_pmax_done")
        w_nmax_done = sem("w_nmax_done")
        w_exp_done = sem("w_exp_done")
        w_rrec_done = sem("w_rrec_done")
        w_p_turned = sem("w_p_turned")
        w_pt_done = sem("w_pt_done")
        w_pt_used = sem("w_pt_used")
        w_a_done = sem("w_a_done")
        w_at_done = sem("w_at_done")
        w_o_done = sem("w_o_done")
        w_z_done = sem("w_z_done")
        w_zneg_done = sem("w_zneg_done")
        w_zpos_done = sem("w_zpos_done")
        w_zexp_done = sem("w_zexp_done")
        w_y_done = sem("w_y_done")
        w_x_done = sem("w_x_done")

        WCH = 512
        WCHUNKS = N // WCH
        WTILES = WCH // P
        wpsS = [bank(0), bank(1)]
        wpsT = [bank(2), bank(3)]

        block = ctx.enter_context(nc.Block())

        def groups(eng, body):
            body(0, True, G == 1)
            if G > 2:
                with eng.Fori(1, G - 1) as g:
                    body(g, False, False)
            if G > 1:
                body(G - 1, False, True)

        def counted(eng, n, body):
            body(0, True)
            with eng.Fori(1, n) as i:
                body(i, False)

        def in_pairs(eng, body):
            body(0, True, G == 2)
            if G > 4:
                with eng.Fori(1, G // 2 - 1) as j:
                    body(j, False, False)
            if G > 2:
                body(G // 2 - 1, False, True)

        @block.sync
        def _(sp):
            for n, w in enumerate((W, Wq, Wk, Wv)):
                sp.dma_start(weights[:, n, :], w).then_inc(consts_in, 16)
            for n, v in enumerate((a[0:D, :], a[D:2 * D, :], col(bq), col(bk))):
                sp.dma_start(cols[:, n:n + 1], v).then_inc(consts_in, 16)
            sp.dma_start(bvrow[0:1, :], bv.rearrange("(o d) -> o d", o=1)).then_inc(consts_in, 16)
            sp.dma_start(X[:, :, :], x_tiles).then_inc(x_in, 16)

            def write_table():
                with sp.Fori(0, G // 2) as j:
                    for k in range(2):
                        sp.wait_ge(h_done, (2 * j + k + 1) * GROUP + T)
                        write_rows(1, 2 * j + k, k)

            def write_rows(layer, g, k):
                sp.dma_start(tables[layer].rearrange("(t p) d -> p t d", p=P)[:, bass.ds(g * GROUP, GROUP), :],
                             stage[:, k, :, :]).then_inc(table_written[k], 16)

            def load_adj(t, q):
                sp.dma_start(adj_sb[:, q, :], adj[bass.ds(t * P, P), q * QUARTER:(q + 1) * QUARTER])\
                  .then_inc(adj_in[q], 16)

            def load_group(g, first, last):
                for b in range(GROUP):
                    t = g * GROUP + b
                    for q in range(QUARTERS):
                        if not (first and b == 0):
                            sp.wait_ge(mask_done, QUARTERS * t - QUARTERS + q + 1)
                        load_adj(t, q)
                    if b == 1 and not first:
                        sp.wait_ge(h_done, g * GROUP)
                        write_rows(0, g - 1, 0)
                if last:
                    sp.wait_ge(h_done, (g + 1) * GROUP)
                    write_rows(0, g, 0)

            groups(sp, load_group)

            sp.wait_ge(flag_done, 1)
            whole = sp.value_load(flag[0:1, 0:1], min_val=0, max_val=1)
            with sp.If(whole > 0):
                for layer in range(2):
                    def load_whole(t, first):
                        for q in range(QUARTERS):
                            if layer or not first:
                                sp.wait_ge(w_adj_used[q], t + layer * T)
                            sp.dma_start(wadj[:, q, :], adj[bass.ds(t * P, P), q * QUARTER:(q + 1) * QUARTER])\
                              .then_inc(w_adj_in[q], 16)

                    counted(sp, T, load_whole)
                sp.wait_ge(w_x_done, 2 * T)
                sp.dma_start(out_tiles, X[:, :, :]).then_inc(out_written, 16)
                sp.wait_ge(out_written, 16)
            with sp.Else():
                write_table()
                with sp.Fori(0, G) as g:
                    sp.wait_ge(x_done, (g + 1) * GROUP + T)
                    sp.dma_start(out_tiles[:, bass.ds(g * GROUP, GROUP), :], X[:, bass.ds(g * GROUP, GROUP), :])\
                      .then_inc(out_written, 16)
                sp.wait_ge(out_written, 16 * G)

        @block.gpsimd
        def _(pool):
            nc.gpsimd.memset(ones[:, :], 1.0).then_inc(pool_consts, 1)
            pool.wait_ge(pool_consts, 1)
            nc.gpsimd.affine_select(out=ident[:, :], in_=ones[:, 0:P], compare_op=ALU.is_equal, fill=0.0, base=0,
                                    pattern=[[-1, P]], channel_multiplier=1).then_inc(pool_consts, 1)
            nc.gpsimd.affine_select(out=scratch[:, 0:P], in_=ones[:, 0:P],
                                    compare_op=ALU.is_ge, fill=0.0, base=0,
                                    pattern=[[1, P]], channel_multiplier=-1).then_inc(pool_consts, 1)
            pool.wait_ge(pool_consts, 3)
            nc.gpsimd.tensor_copy(upto[:, :], scratch[:, 0:P]).then_inc(pool_consts, 1)
            nc.gpsimd.memset(eps[:, :], EPS).then_inc(pool_consts, 1)
            nc.gpsimd.memset(ones16[:, :], 1.0).then_inc(pool_consts, 1)
            nc.gpsimd.memset(mix[:, 0, :], 0.0).then_inc(pool_consts, 1)
            nc.gpsimd.memset(mix_bias[:, 0, :], 0.0).then_inc(pool_consts, 1)
            nc.gpsimd.memset(obias[:, 0, :], 0.0).then_inc(pool_consts, 1)
            nc.gpsimd.memset(mask[:, :, N:SEGS * BLOCK] if SEGS * BLOCK > N else mask[:, :, 0:1], 0.0)\
              .then_inc(pool_consts, 1)
            small = dict(channel_multiplier=0, allow_small_or_imprecise_dtypes=True)
            nc.gpsimd.iota(iota_slot[:, :], pattern=[[1, SLOTS]], base=0, **small).then_inc(pool_consts, 1)
            nc.gpsimd.iota(iota_row[:, :], pattern=[[1, P]], base=1, **small).then_inc(pool_consts, 1)
            nc.gpsimd.iota(iota_q[:, :], pattern=[[P, CHUNKS]], base=0, channel_multiplier=1,
                           allow_small_or_imprecise_dtypes=True).then_inc(pool_consts, 1)
            pool.wait_ge(pool_consts, 4)
            nc.gpsimd.iota(scratch[:, :], pattern=[[1, QCOLS]], base=0, **small).then_inc(pool_consts, 1)
            pool.wait_ge(pool_consts, 14)
            nc.gpsimd.tensor_copy(iota16[:, :], scratch[:, :]).then_inc(pool_consts, 1)
            B64 = BLOCK // 64 + 1
            pool.wait_ge(pool_consts, 15)
            nc.gpsimd.iota(scratch[:, 0:64 * B64], pattern=[[64, B64], [0, 64]], base=0, **small).then_inc(pool_consts, 1)
            pool.wait_ge(pool_consts, 16)
            nc.gpsimd.tensor_copy(place_hi[:, 0:BLOCK], scratch[:, 0:BLOCK]).then_inc(pool_consts, 1)
            pool.wait_ge(pool_consts, 17)
            nc.gpsimd.iota(scratch[:, 0:64 * B64], pattern=[[0, B64], [1, 64]], base=0, **small).then_inc(pool_consts, 1)
            pool.wait_ge(pool_consts, 18)
            nc.gpsimd.tensor_copy(place_lo[:, 0:BLOCK], scratch[:, 0:BLOCK]).then_inc(pool_consts, 1)
            pool.wait_ge(pool_consts, 19)
            nc.gpsimd.iota(scratch[:, 0:1], pattern=[[0, 1]], base=1, channel_multiplier=1,
                           allow_small_or_imprecise_dtypes=True).then_inc(pool_consts, 1)
            pool.wait_ge(pool_consts, 20)
            for b in range(GROUP):
                nc.gpsimd.tensor_copy(hi16[:, b, SLOTS + 1:SLOTS + 2], scratch[:, 0:1]).then_inc(pool_consts, 1)
                nc.gpsimd.memset(lo16[:, b, SLOTS + 1:SLOTS + 2], 0.0).then_inc(pool_consts, 1)

            pool.wait_ge(flag_done, 1)
            whole = pool.value_load(flag[0:1, 0:1], min_val=0, max_val=1)
            with pool.If(whole > 0):
                for layer in range(2):
                    with pool.Fori(0, WCHUNKS) as i:
                        pool.wait_ge(w_h_done, (i + 1) * WTILES + layer * T)
                        nc.gpsimd.tensor_copy(wH[:, bass.ds(i * WTILES, WTILES), :], wstage[:, :, :]).then_inc(w_h_kept, 1)
                    pool.wait_ge(w_ht_done, (layer + 1) * WCHUNKS)
                    def copy_rows(i, first):
                        if layer or not first:
                            pool.wait_ge(w_u_done, i + layer * T)
                        nc.gpsimd.tensor_copy(wrows[:, :], wHT[:, bass.ds(i * P, P)]).then_inc(w_rows_done, 1)

                    counted(pool, T, copy_rows)
            with pool.Else():
                nc.gpsimd.memset(Gt[:, :, :, :], 1.0).then_inc(pool_consts, 1)
                pool.wait_ge(pool_consts, 21 + 2 * GROUP)
                for layer in range(2):
                    pool.wait_ge(table_written[0], 16 * G + 8 * G * layer)
                    if layer:
                        pool.wait_ge(table_written[1], 8 * G)

                    def gather_group(g, first, last, layer=layer):
                        for b in range(GROUP):
                            tt = g * GROUP + b + layer * T
                            if not (first and layer == 0):
                                pool.wait_ge(acc_done, tt - GROUP + 1)
                            nc.gpsimd.tensor_copy(idx_now[:, b:b + 1, :], idx_all[:, bass.ds(g * GROUP + b, 1), :])\
                              .then_inc(idx_done, 1)
                            pool.wait_ge(idx_done, tt + 1)
                            pool.sem_inc(gathering, 1)
                            for c in range(CHUNKS):
                                pool.indirect_dma_start(Gt[:, b, c, 0:D], None, tables[layer],
                                                        bass.IndirectOffsetOnAxis(idx_now[:, b, c:c + 1], 0),
                                                        bounds_check=N - 1, oob_is_err=False).then_inc(rows_in[b], 16)

                    groups(pool, gather_group)

        @block.vector
        def _(dve):
            dve.wait_ge(consts_in, 16 * 9)
            dve.wait_ge(pool_consts, 20 + 2 * GROUP)
            nc.vector.tensor_scalar(spread[:, 0, :], ones[:, 0:D], bq_c, None, ALU.mult).then_inc(spread_done, 1)
            nc.vector.tensor_scalar(spread[:, 1, :], ones[:, 0:D], a2_c, None, ALU.mult).then_inc(spread_done, 1)
            nc.vector.tensor_copy(wk_bk[:, 0:D], wk_sb).then_inc(spread_done, 1)
            nc.vector.tensor_copy(wk_bk[:, D:DE], bk_c).then_inc(spread_done, 1)
            nc.vector.tensor_copy(iota_row16[:, :], iota_row[:, :]).then_inc(dve_consts, 1)
            nc.vector.tensor_copy(ident16[:, :], ident[:, :]).then_inc(dve_consts, 1)
            for s in range(SEGS):
                nc.vector.tensor_scalar(shifted[:, s, :], ident[:, :], float(2 ** (s + PLACE_BITS)), None, ALU.mult)\
                  .then_inc(dve_consts, 1)
            dve.wait_ge(w_turned, 2)
            nc.vector.tensor_copy(wT[:, :, :], bank(0)[:, 0:2 * D].rearrange("p (n d) -> p n d", n=2))\
              .then_inc(w_turned_sb, 1)
            dve.wait_ge(mixed, 1)
            nc.vector.tensor_copy(mix[:, 0, D:DE], bank(1)[:, 0:1]).then_inc(mixed_sb, 1)
            nc.vector.tensor_copy(mix_bias[:, 0, 0:D], bank(1)[:, 128:256]).then_inc(mixed_sb, 1)
            nc.vector.tensor_copy(mix[:, 1, :], bank(2)[:, 0:DE]).then_inc(mixed_sb, 1)
            nc.vector.tensor_copy(mix_bias[:, 1, :], bank(3)[:, 0:DE]).then_inc(mixed_sb, 1)
            nc.vector.tensor_copy(mix_col[:, 0:1], bank(1)[:, 1:2]).then_inc(mixed_sb, 1)
            nc.vector.tensor_copy(mix_col[:, 1:2], bank(1)[:, 2:3]).then_inc(mixed_sb, 1)
            nc.vector.tensor_copy(obias[:, 1, :], bank(1)[:, 256:384]).then_inc(mixed_sb, 1)
            nc.vector.tensor_copy(proj[:, 0, :], w_sb).then_inc(mixed_sb, 1)
            nc.vector.tensor_copy(proj[:, 1, :], wT[:, 1, :]).then_inc(mixed_sb, 1)

            MEASURED = 8

            def moments(nth, measure=True):
                if measure:
                    with dve.Fori(0, T // MEASURED) as i:
                        for n in range(MEASURED):
                            at = bass.ds(i * MEASURED + n, 1)
                            nc.vector.bn_stats(stats[:, at, :], X[:, at, :]).then_inc(stats_done, 1)
                dve.wait_ge(stats_done, nth * T)
                nc.vector.tensor_tensor(half_gap[:, :], stats[:, :, 1], stats[:, :, 4], ALU.subtract).then_inc(gap_done, 1)
                nc.vector.tensor_tensor(mean[:, :], stats[:, :, 1], stats[:, :, 4], ALU.add).then_inc(mean_done, 1)
                nc.vector.tensor_tensor(var[:, :], stats[:, :, 2], stats[:, :, 5], ALU.add).then_inc(var_done, 1)
                dve.wait_ge(gap_done, 3 * nth - 2)
                nc.vector.tensor_tensor(half_gap[:, :], half_gap[:, :], half_gap[:, :], ALU.mult).then_inc(gap_done, 1)
                dve.wait_ge(gap_done, 3 * nth - 1)
                nc.vector.tensor_scalar(half_gap[:, :], half_gap[:, :], 0.25, None, ALU.mult).then_inc(gap_done, 1)
                dve.wait_ge(gap_done, 3 * nth)
                dve.wait_ge(var_done, 2 * nth - 1)
                nc.vector.scalar_tensor_tensor(out=var[:, :], in0=var[:, :], scalar=1.0 / D, in1=half_gap[:, :],
                                               op0=ALU.mult, op1=ALU.add).then_inc(var_done, 1)
                dve.wait_ge(sd_done, nth)
                nc.vector.reciprocal(rstd[:, :], sd[:, :]).then_inc(rstd_done, 1)
                dve.wait_ge(rstd_done, nth)
                dve.wait_ge(mean_done, nth)
                nc.vector.scalar_tensor_tensor(out=shift[:, :], in0=mean[:, :], scalar=-0.5, in1=rstd[:, :],
                                               op0=ALU.mult, op1=ALU.mult).then_inc(shift_done, 1)

            def keep_rows(g, k, layer):
                dve.wait_ge(h_turned, g + 1 + layer * G)
                nc.vector.tensor_copy(stageT[:, k, :], (bank(k) if layer else bank(7))[:, :]).then_inc(ht_done, 1)

            def keep_u(g, n, ps, layer):
                nc.vector.tensor_tensor(U[:, bass.ds(g * GROUP + 2 * n, 2), :],
                                        ps.rearrange("p (a d) -> p a d", a=2)[:, :, 0:DE],
                                        mix_bias[:, layer:layer + 1, :].to_broadcast([P, 2, DE]), ALU.add)\
                  .then_inc(u_kept, 1)

            def keep_layer():
                def pair(j, first, last):
                    for k in range(2):
                        g = 2 * j + k
                        keep_rows(g, k, 1)
                        if not (first and k == 0):
                            leave(g - 1, (k + 1) % 2)
                    if last:
                        leave(g, k)

                def leave(g, k):
                    dve.wait_ge(u_done, g + 1 + 2 * G)
                    for n in range(2):
                        keep_u(g, n, bank(2 + 2 * k + n), 1)

                in_pairs(dve, pair)

            dve.wait_ge(x_in, 16)
            moments(1)

            def extract(g, b):
                t = g * GROUP + b
                v = V[b % 2]
                dve.wait_ge(packed, t + 1)
                dve.sem_inc(in_step, 1)
                nc.vector.max(words[:, b, 0:8], v).then_inc(top_done, 1)
                dve.wait_ge(top_done, 3 * t + 1)
                dve.sem_inc(in_step, 1)
                nc.vector.match_replace(rest[:, 0, :], words[:, b, 0:8], v, 0.0).then_inc(rest_done, 1)
                dve.wait_ge(rest_done, 2 * t + 1)
                dve.sem_inc(in_step, 1)
                nc.vector.max(words[:, b, 8:16], rest[:, 0, :]).then_inc(top_done, 1)
                dve.wait_ge(top_done, 3 * t + 2)
                dve.sem_inc(in_step, 1)
                nc.vector.match_replace(rest[:, 1, :], words[:, b, 8:16], rest[:, 0, :], 0.0).then_inc(rest_done, 1)
                dve.wait_ge(rest_done, 2 * t + 2)
                dve.sem_inc(in_step, 1)
                nc.vector.max(words[:, b, 16:24], rest[:, 1, :]).then_inc(top_done, 1)

            flat = words.rearrange("p b k -> p (b k)")
            DECODE = 13

            def decode(g):
                step = [0]

                def done(ins):
                    ins.then_inc(decoded, 1)
                    step[0] += 1

                def after(n=None):
                    dve.wait_ge(decoded, DECODE * g + (step[0] if n is None else n))

                dve.wait_ge(top_done, 3 * GROUP * (g + 1))
                done(nc.vector.tensor_copy(words_i[:, :], flat))
                nc.vector.tensor_copy(widest_all[:, bass.ds(g * GROUP, GROUP)], words[:, :, 0]).then_inc(lists_done, 1)
                after()
                done(nc.vector.tensor_single_scalar(place_i[:, :], words_i[:, :], 2 ** PLACE_BITS - 1, ALU.bitwise_and))
                done(nc.vector.tensor_single_scalar(bits_i[:, :], words_i[:, :], PLACE_BITS, ALU.arith_shift_right))
                after(3)
                done(nc.vector.tensor_scalar(place_f[:, :], place_i[:, :], float(1 - 127 * BLOCK), None, ALU.add))
                done(nc.vector.tensor_copy(bits_f[:, 0, :], bits_i[:, :]))
                for n in range(DEPTH):
                    after()
                    done(nc.vector.tensor_single_scalar(top_f[:, n, :].bitcast(I32), bits_f[:, n, :].bitcast(I32),
                                                        0x7F800000, ALU.bitwise_and))
                    if n + 1 < DEPTH:
                        after()
                        done(nc.vector.tensor_tensor(bits_f[:, n + 1, :], bits_f[:, n, :], top_f[:, n, :], ALU.subtract))
                after()
                done(nc.vector.tensor_single_scalar(expo_i[:, :, :], top_f[:, :, :].bitcast(I32), 23,
                                                    ALU.arith_shift_right))
                after()
                done(nc.vector.scalar_tensor_tensor(
                    out=node_f[:, :, :], in0=expo_i[:, :, :], scalar=float(BLOCK),
                    in1=place_f[:, :].rearrange("p (o k) -> p o k", o=1).to_broadcast([P, DEPTH, GROUP * WORDS]),
                    op0=ALU.mult, op1=ALU.add))
                after()
                done(nc.vector.scalar_tensor_tensor(
                    out=found.rearrange("p n b k -> p (n b k)"), in0=top_f.rearrange("p n k -> p (n k)"), scalar=0.0,
                    in1=node_f.rearrange("p n k -> p (n k)"), op0=ALU.is_gt, op1=ALU.mult))
                assert step[0] == DECODE, step
                after()
                for b in range(GROUP):
                    t = g * GROUP + b
                    now, k = found[:, :, b, :], 0
                    while True:
                        dve.sem_inc(in_step, 1)
                        nc.vector.max(listed[:, b, 8 * k:8 * k + 8], now).then_inc(ltop_done, 1)
                        k += 1
                        if 8 * k == SLOTS:
                            break
                        dve.wait_ge(ltop_done, (SLOTS // 8) * t + k)
                        dve.sem_inc(in_step, 1)
                        nxt = found2[:, (k - 1) % 2, :].rearrange("p (n k) -> p n k", n=DEPTH)
                        nc.vector.match_replace(nxt, listed[:, b, 8 * k - 8:8 * k], now, 0.0).then_inc(lrest_done, 1)
                        dve.wait_ge(lrest_done, (SLOTS // 8 - 1) * t + k)
                        now = nxt
                dve.wait_ge(ltop_done, (SLOTS // 8) * GROUP * (g + 1))
                nc.vector.tensor_scalar(is_listed[:, :, :], listed[:, :, 0:SLOTS], 0.0, None, ALU.is_gt).then_inc(count_done, 1)
                dve.wait_ge(count_done, 3 * g + 1)
                nc.vector.tensor_reduce(count4[:, :], is_listed[:, :, :], AX.X, ALU.add).then_inc(count_done, 1)
                dve.wait_ge(count_done, 3 * g + 2)
                nc.vector.tensor_copy(count_all[:, bass.ds(g * GROUP, GROUP)], count4[:, :]).then_inc(lists_done, 1)
                nc.vector.tensor_copy(count16[:, :], count4[:, :]).then_inc(count_done, 1)

            def split(g):
                dve.wait_ge(ends_done, g + 1)
                nc.vector.tensor_copy(end4[:, :], bank(6)[:, 0:GROUP]).then_inc(split_done, 1)
                dve.wait_ge(split_done, 6 * g + 1)
                nc.vector.tensor_copy(end_all[:, bass.ds(g * GROUP, GROUP)], end4[:, :]).then_inc(lists_done, 1)
                nc.vector.tensor_tensor(listed[:, :, SLOTS], end4[:, :], count4[:, :], ALU.subtract).then_inc(split_done, 1)
                dve.wait_ge(split_done, 6 * g + 2)
                nc.vector.tensor_copy(listed_i[:, :], listed.rearrange("p b k -> p (b k)")).then_inc(split_done, 1)
                dve.wait_ge(split_done, 6 * g + 3)
                nc.vector.tensor_single_scalar(lo_i[:, :], listed_i[:, :], 63, ALU.bitwise_and).then_inc(split_done, 1)
                dve.wait_ge(split_done, 6 * g + 4)
                low = lo_i.rearrange("p (b k) -> p b k", b=GROUP)
                nc.vector.tensor_copy(lo16[:, :, 0:SLOTS + 1], low).then_inc(split_done, 1)
                nc.vector.tensor_tensor(hi16[:, :, 0:SLOTS + 1], listed[:, :, :], low, ALU.subtract).then_inc(split_done, 1)

            def mark(g, b):
                t = g * GROUP + b
                nc.vector.tensor_scalar(from_pre[:, :], iota16[:, :], listed[:, b, SLOTS:SLOTS + 1], None, ALU.is_ge)\
                  .then_inc(mine_done, 1)
                nc.vector.tensor_scalar(from_end[:, :], iota16[:, :], end4[:, b:b + 1], None, ALU.is_ge)\
                  .then_inc(mine_done, 1)
                dve.wait_ge(mine_done, 3 * t + 2)
                nc.vector.tensor_tensor(mine[:, b % 2, :], from_pre[:, :], from_end[:, :], ALU.subtract)\
                  .then_inc(mine_done, 1)
                dve.wait_ge(mine_done, 3 * t + 3)

            def pick(g, b):
                t = g * GROUP + b
                ps = q_lists[b % 2]
                at = bass.ds(t, 1)
                wide = lambda v: v.to_broadcast([P, CHUNKS, SLOTS])
                dve.wait_ge(q_done, t + 1)
                nc.vector.tensor_tensor(slot_all[:, at, :], iota_q.rearrange("p (o c) -> p o c", o=1),
                                        ps[:, :, SLOTS].rearrange("p (o c) -> p o c", o=1), ALU.subtract)\
                  .then_inc(pick_done, 1)
                nc.vector.tensor_copy(owner_all[:, at, :], ps[:, :, SLOTS + 1].rearrange("p (o c) -> p o c", o=1))\
                  .then_inc(lists_done, 1)
                dve.wait_ge(pick_done, 6 * t + 1)
                nc.vector.tensor_tensor(one_hot[:, :, :], wide(iota_slot.rearrange("p (o k) -> p o k", o=1)),
                                        wide(slot_all[:, at, :].rearrange("p o c -> p c o")), ALU.is_equal)\
                  .then_inc(pick_done, 1)
                dve.wait_ge(pick_done, 6 * t + 2)
                nc.vector.tensor_tensor(picked[:, :, :], ps[:, :, 0:SLOTS], one_hot[:, :, :], ALU.mult).then_inc(pick_done, 1)
                dve.wait_ge(pick_done, 6 * t + 3)
                nc.vector.tensor_reduce(node_q[:, :], picked[:, :, :], AX.X, ALU.add).then_inc(pick_done, 1)
                dve.wait_ge(pick_done, 6 * t + 4)
                nc.vector.tensor_scalar(past_q[:, :], node_q[:, :], 0.0, float(2 * N), ALU.is_equal, ALU.mult)\
                  .then_inc(pick_done, 1)
                dve.wait_ge(pick_done, 6 * t + 5)
                nc.vector.scalar_tensor_tensor(out=idx_all[:, at, :], in0=node_q.rearrange("p (o c) -> p o c", o=1),
                                               scalar=-1.0, in1=past_q.rearrange("p (o c) -> p o c", o=1),
                                               op0=ALU.add, op1=ALU.add).then_inc(pick_done, 1)

            def survey_group(g, first, last):
                for b in range(GROUP):
                    extract(g, b)
                    if not first:
                        if b == 0:
                            split(g - 1)
                            dve.wait_ge(split_done, 6 * g)
                            mark(g - 1, 0)
                        else:
                            pick(g - 1, b - 1)
                        if b + 1 < GROUP:
                            mark(g - 1, b + 1)
                    if b == 2:
                        keep_rows(g, 0, 0)
                    if b == 3:
                        dve.wait_ge(u_done, 2 * g + 1)
                        keep_u(g, 0, bank(7), 0)
                if not first:
                    pick(g - 1, GROUP - 1)
                dve.wait_ge(u_done, 2 * g + 2)
                keep_u(g, 1, bank(7), 0)
                decode(g)
                if last:
                    split(g)
                    dve.wait_ge(split_done, 6 * (g + 1))
                    for b in range(GROUP):
                        mark(g, b)
                        if b:
                            pick(g, b - 1)
                    pick(g, GROUP - 1)

            groups(dve, survey_group)

            dve.wait_ge(lists_done, 3 * G + T)
            dve.wait_ge(mask_done, QUARTERS * T)
            nc.vector.tensor_reduce(half_gap[:, :], sum_all[:, :, :], AX.X, ALU.add).then_inc(bad_done, 1)
            dve.wait_ge(bad_done, 1)
            nc.vector.tensor_tensor(half_gap[:, :], half_gap[:, :], count_all[:, :], ALU.not_equal).then_inc(bad_done, 1)
            dve.wait_ge(bad_done, 2)
            nc.vector.tensor_reduce(bad[:, 0:1], half_gap[:, :], AX.X, ALU.max).then_inc(bad_done, 1)
            nc.vector.tensor_scalar(var[:, :], widest_all[:, :], float(EXACT) - 1.0, None, ALU.is_gt).then_inc(bad_done, 1)
            dve.wait_ge(bad_done, 4)
            nc.vector.tensor_reduce(bad[:, 1:2], var[:, :], AX.X, ALU.max).then_inc(bad_done, 1)
            nc.vector.tensor_scalar(sd[:, :], end_all[:, :], float(QCOLS), None, ALU.is_gt).then_inc(bad_done, 1)
            dve.wait_ge(bad_done, 6)
            nc.vector.tensor_reduce(bad[:, 2:3], sd[:, :], AX.X, ALU.max).then_inc(bad_done, 1)
            nc.vector.tensor_scalar(mean[:, :], count_all[:, :], 1.0, None, ALU.is_lt).then_inc(bad_done, 1)
            dve.wait_ge(bad_done, 8)
            nc.vector.tensor_reduce(bad[:, 3:4], mean[:, :], AX.X, ALU.max).then_inc(bad_done, 1)
            dve.wait_ge(bad_done, 9)
            nc.vector.tensor_reduce(bad_row[:, :], bad[:, :], AX.X, ALU.max).then_inc(bad_done, 1)
            dve.wait_ge(table_written[0], 16 * G)
            dve.wait_ge(bad_summed, 1)
            nc.vector.tensor_scalar(flag[0:1, :], bank(7)[0:1, 0:1], 0.5, None, ALU.is_gt).then_inc(flag_done, 1)
            dve.wait_ge(flag_done, 1)
            whole = dve.value_load(flag[0:1, 0:1], min_val=0, max_val=1)

            with dve.If(whole > 0):
                for layer in range(2):
                    base = layer * T
                    if layer:
                        dve.wait_ge(w_x_done, T)
                        moments(2)
                    with dve.Fori(0, WCHUNKS) as i:
                        dve.wait_ge(w_h_turned, i + 1 + layer * WCHUNKS)
                        nc.vector.tensor_copy(wHT[:, bass.ds(i * WCH, WCH)], wpsT[0]).then_inc(w_ht_done, 1)

                    with dve.Fori(0, T) as i:
                        t = i + base
                        dve.wait_ge(w_u_done, t + 1)
                        nc.vector.tensor_scalar(wcbias[:, :], bank(7)[:, 0:1], mix_bias[:, layer, D:DE],
                                                1.0 if layer == 0 else SCALE, ALU.add, ALU.mult).then_inc(w_cbias_done, 1)
                        for q in range(QUARTERS):
                            piece = wS[:, q * QUARTER:(q + 1) * QUARTER]
                            dve.wait_ge(w_s_moved, WCHUNKS * t + -(-(q + 1) * QUARTER // WCH))
                            if layer == 0:
                                nc.vector.scalar_tensor_tensor(out=piece, in0=piece, scalar=ALPHA, in1=piece,
                                                               op0=ALU.mult, op1=ALU.max).then_inc(w_leaky_done, 1)
                            if q:
                                dve.wait_ge(w_masked, QUARTERS * t + q)
                            dve.wait_ge(w_adj_in[q], 16 * t + 16)
                            nc.vector.tensor_scalar(penalty[:, :], wadj[:, q, :], 0.0, NEG, ALU.is_le, ALU.mult)\
                              .then_inc(w_penalty_done, 1)
                            if layer == 0:
                                dve.wait_ge(w_leaky_done, QUARTERS * t + q + 1)
                            dve.wait_ge(w_penalty_done, QUARTERS * t + q + 1)
                            dve.sem_inc(w_adj_used[q], 1)
                            nc.vector.tensor_tensor_reduce(out=piece, in0=piece, in1=penalty[:, :], scale=1.0,
                                                           scalar=-3.0e38, op0=ALU.add, op1=ALU.max,
                                                           accum_out=wpmax[:, q:q + 1]).then_inc(w_masked, 1)
                        dve.wait_ge(w_masked, QUARTERS * t + QUARTERS)
                        nc.vector.tensor_reduce(wnmax[:, :], wpmax[:, :], AX.X, ALU.max).then_inc(w_pmax_done, 1)
                        dve.wait_ge(w_pmax_done, t + 1)
                        nc.vector.tensor_scalar(wnmax[:, :], wnmax[:, :], -1.0, None, ALU.mult).then_inc(w_nmax_done, 1)
                        dve.wait_ge(w_exp_done, t + 1)
                        nc.vector.reciprocal(wrrec[:, :], wrsum[:, :]).then_inc(w_rrec_done, 1)
                        dve.wait_ge(w_a_done, t + 1)
                        nc.vector.tensor_copy(wAT[:, :], bank(4)[:, 0:P]).then_inc(w_at_done, 1)
                        dve.wait_ge(w_rrec_done, t + 1)
                        dve.wait_ge(w_o_done, t + 1)
                        nc.vector.scalar_tensor_tensor(out=wz[:, :], in0=bank(5)[:, 0:D], scalar=wrrec[:, 0:1],
                                                       in1=obias[:, layer, :], op0=ALU.mult, op1=ALU.add).then_inc(w_z_done, 1)
                        dve.wait_ge(w_z_done, t + 1)
                        nc.vector.tensor_scalar(wzneg[:, :], wz[:, :], 0.0, None, ALU.min).then_inc(w_zneg_done, 1)
                        nc.vector.tensor_scalar(wzpos[:, :], wz[:, :], 0.0, -1.0, ALU.max, ALU.add).then_inc(w_zpos_done, 1)
                        dve.wait_ge(w_zexp_done, t + 1)
                        dve.wait_ge(w_zpos_done, t + 1)
                        nc.vector.tensor_tensor(wzpos[:, :], wzpos[:, :], wzexp[:, :], ALU.add).then_inc(w_y_done, 1)
                        dve.wait_ge(w_y_done, t + 1)
                        nc.vector.tensor_tensor(X[:, bass.ds(i, 1), :], X[:, bass.ds(i, 1), :],
                                                wzpos.rearrange("p (o d) -> p o d", o=1), ALU.add).then_inc(w_x_done, 1)
            with dve.Else():
                for layer in range(2):
                    base = layer * T
                    if layer:
                        moments(2, False)
                        keep_layer()
                    wide_p = lambda v: v.to_broadcast([P, CHUNKS, P])
                    wide_k = lambda v: v.to_broadcast([P, CHUNKS, SLOTS])
                    cut = lambda v: v.rearrange("p (c o) -> p c o", o=1)

                    def own(t, b):
                        for c in range(CHUNKS):
                            last_one = nc.vector.tensor_scalar(
                                owned[:, b % GROUP, c, :], iota_row16[:, :],
                                owner_all[:, bass.ds(t, 1), c:c + 1].rearrange("p o c -> p (o c)"), None, ALU.is_equal)
                        last_one.then_inc(owned_done, 1)

                    def hot(t, b):
                        nc.vector.tensor_tensor(slot_hot[:, b % GROUP, :, :], wide_k(iota_slot.rearrange("p (o k) -> p o k", o=1)),
                                                wide_k(slot_all[:, bass.ds(t, 1), :].rearrange("p o c -> p c o")),
                                                ALU.is_equal).then_inc(hot_done, 1)

                    def products(g, b):
                        t = g * GROUP + b
                        tt = t + base
                        nc.vector.tensor_scalar(pad[:, :], iota_slot[:, :], count_all[:, bass.ds(t, 1)], NEG,
                                                ALU.is_ge, ALU.mult).then_inc(pad_done, 1)
                        dve.wait_ge(rows_in[b % GROUP], (g + b // GROUP + 1 + layer * G) * 16 * CHUNKS)
                        for u, (c0, c1) in enumerate(spread_parts):
                            if u < SPREADS - 1:
                                dve.wait_ge(spread_u, (SPREADS - 1) * tt + u + 1)
                            else:
                                dve.wait_ge(scattered, tt + layer + 1)
                            nc.vector.tensor_tensor(prod[:, c0:c1, :], spread_ps[u], Gt[:, b % GROUP, c0:c1, :],
                                                    ALU.mult).then_inc(prod_done, 1)

                    def scores(t, b):
                        tt = t + base
                        dve.wait_ge(prod_done, SPREADS * (tt + 1))
                        nc.vector.tensor_reduce(raw[:, :], prod[:, :, :], AX.X, ALU.add).then_inc(raw_done, 1)
                        dve.wait_ge(raw_done, tt + 1)
                        for to in (score[:, b % 2, :], score16[:, 0, :]):
                            if layer == 0:
                                nc.vector.scalar_tensor_tensor(out=to, in0=raw[:, :], scalar=ALPHA, in1=raw[:, :],
                                                               op0=ALU.mult, op1=ALU.max).then_inc(score_done, 1)
                            else:
                                nc.vector.tensor_scalar(to, raw[:, :], SCALE, None, ALU.mult).then_inc(score_done, 1)
                        dve.wait_ge(score_done, 3 * tt + 2)
                        nc.vector.tensor_tensor(score16[:, 1, :], score[:, b % 2, :], score16[:, 0, :], ALU.subtract)\
                          .then_inc(score_done, 1)
                        dve.wait_ge(score_done, 3 * tt + 3)
                        dve.wait_ge(hot_done, tt + 1)
                        nc.vector.tensor_tensor(
                            slot_e[:, :, :, :],
                            slot_hot[:, b % GROUP:b % GROUP + 1, :, :].to_broadcast([P, 2, CHUNKS, SLOTS]),
                            score16.rearrange("p n (c o) -> p n c o", o=1).to_broadcast([P, 2, CHUNKS, SLOTS]),
                            ALU.mult).then_inc(slot_e_done, 1)

                    def maxima(t, b):
                        tt = t + base
                        dve.wait_ge(scattered, tt + layer + 2)
                        dve.wait_ge(pad_done, tt + 1)
                        nc.vector.tensor_tensor(by_slot[:, :], by_slot_ps, pad[:, :], ALU.add).then_inc(by_slot_done, 1)
                        dve.wait_ge(by_slot_done, tt + 1)
                        for to in (row_max[:, :], max16[:, 0:1]):
                            nc.vector.tensor_reduce(to, by_slot[:, :], AX.X, ALU.max).then_inc(max_done, 1)
                        dve.wait_ge(max_done, 3 * tt + 2)
                        nc.vector.tensor_tensor(max16[:, 1:2], row_max[:, :], max16[:, 0:1], ALU.subtract).then_inc(max_done, 1)

                    def below(t, b):
                        tt = t + base
                        dve.wait_ge(max_spread, tt + 1)
                        nc.vector.tensor_tensor(gap[:, :], score[:, b % 2, :], max_ps, ALU.subtract).then_inc(below_done, 1)

                    def weigh(t, b):
                        tt = t + base
                        dve.wait_ge(prob_done, tt + 1)
                        nc.vector.tensor_tensor(weighted[:, b % 2, :, :], owned[:, b % GROUP, :, :], wide_p(cut(prob)), ALU.mult)\
                          .then_inc(weighted_done, 1)

                    def inverse(t, b):
                        dve.wait_ge(acc_done, t + base + 1)
                        nc.vector.reciprocal(rsum[:, :], bank(6)[:, D:DE]).then_inc(rsum_done, 1)

                    def finish(t, b):
                        tt = t + base
                        dve.wait_ge(o_done, tt + 1)
                        nc.vector.tensor_tensor(z[:, :], bank(7)[:, 0:D], obias[:, layer, :], ALU.add).then_inc(z_done, 1)
                        dve.wait_ge(z_done, tt + 1)
                        nc.vector.tensor_scalar(zneg[:, :], z[:, :], 0.0, None, ALU.min).then_inc(zneg_done, 1)

                    def finish2(t, b):
                        tt = t + base
                        dve.wait_ge(zexp_done, tt + 1)
                        nc.vector.scalar_tensor_tensor(out=y[:, :], in0=z[:, :], scalar=0.0, in1=zexp[:, :],
                                                       op0=ALU.max, op1=ALU.add).then_inc(y_done, 1)
                        dve.wait_ge(y_done, tt + 1)
                        at = bass.ds(t, 1)
                        nc.vector.scalar_tensor_tensor(out=X[:, at, :], in0=y.rearrange("p (o d) -> p o d", o=1), scalar=-1.0,
                                                       in1=X[:, at, :], op0=ALU.add, op1=ALU.add).then_inc(x_done, 1)

                    def measure(t):
                        dve.wait_ge(x_done, t + 1)
                        nc.vector.bn_stats(stats[:, bass.ds(t, 1), :], X[:, bass.ds(t, 1), :]).then_inc(stats_done, 1)

                    def attend_group(g, first, last):
                        if first:
                            for b in range(3):
                                own(b, b)
                                hot(b, b)
                            products(0, 0)
                            scores(0, 0)
                            maxima(0, 0)
                        for b in range(GROUP):
                            t = g * GROUP + b
                            before = not (first and b == 0)
                            after = not (last and b == GROUP - 1)
                            after3 = not (last and b >= GROUP - 3)
                            below(t, b)
                            if after:
                                products(g, b + 1)
                                scores(t + 1, b + 1)
                            if before:
                                inverse(t - 1, b - 1)
                            if after3:
                                own(t + 3, b + 3)
                            if layer == 0 and not (first and b < 2):
                                measure(t - 2)
                            if before:
                                finish(t - 1, b - 1)
                            if after:
                                maxima(t + 1, b + 1)
                            weigh(t, b)
                            if after3:
                                hot(t + 3, b + 3)
                            if before:
                                finish2(t - 1, b - 1)
                        if last:
                            inverse(t, b)
                            finish(t, b)
                            finish2(t, b)
                            if layer == 0:
                                measure(t - 1)
                                measure(t)

                    groups(dve, attend_group)

        @block.scalar
        def _(act):
            def sd_of(nth):
                act.wait_ge(var_done, 2 * nth)
                nc.scalar.activation(sd[:, :], var[:, :], ACT.Sqrt, bias=eps[:, 0:1]).then_inc(sd_done, 1)
                act.wait_ge(shift_done, nth)

            def rows_h(m, to, signal):
                nc.scalar.activation(to, X[:, bass.ds(m, 1), :], ACT.Relu, bias=shift[:, bass.ds(m, 1)],
                                     scale=rstd[:, bass.ds(m, 1)]).then_inc(signal, 1)

            def stage_h():
                def pair(j, first, last):
                    for k in range(2):
                        g = 2 * j + k
                        if k == 0:
                            act.wait_ge(table_written[k], 16 * j + 16 * G)
                            act.wait_ge(h_turned, G if first else g - 1 + G)
                        elif not first:
                            act.wait_ge(table_written[k], 16 * j)
                            act.wait_ge(h_turned, g - 1 + G)
                        for b in range(GROUP):
                            rows_h(g * GROUP + b, stage[:, k, b:b + 1, :], h_done)

                in_pairs(act, pair)

            act.wait_ge(pool_consts, 20 + 2 * GROUP)

            def relu_tile(t, b, wait_packed):
                if wait_packed:
                    act.wait_ge(packed, t - 1)
                for q in range(QUARTERS):
                    act.wait_ge(adj_in[q], 16 * t + 16)
                    nc.scalar.activation(mask[:, b % 2, q * QUARTER:(q + 1) * QUARTER], adj_sb[:, q, :], ACT.Relu,
                                         accum_out=sum_all[:, bass.ds(t, 1), q:q + 1].rearrange("p o c -> p (o c)"))\
                      .then_inc(mask_done, 1)

            def relu_group(g, first, last):
                for b in range(GROUP):
                    relu_tile(g * GROUP + b, b, not (first and b < 2))
                    if first and b == 1:
                        sd_of(1)
                    if b == 2:
                        if not first:
                            act.wait_ge(table_written[0], 16 * g)
                            act.wait_ge(h_turned, g)
                        for n in range(GROUP):
                            rows_h(g * GROUP + n, stage[:, 0, n:n + 1, :], h_done)

            groups(act, relu_group)

            act.wait_ge(flag_done, 1)
            whole = act.value_load(flag[0:1, 0:1], min_val=0, max_val=1)
            with act.If(whole > 0):
                for layer in range(2):
                    base = layer * T

                    def freed(i, layer=layer):
                        act.wait_ge(w_h_kept, i + layer * WCHUNKS)
                        act.wait_ge(w_h_turned, i + layer * WCHUNKS)

                    if layer:
                        sd_of(2)

                    def stage_group(g, first, last):
                        if layer or not first:
                            freed(g)
                        for b in range(GROUP):
                            rows_h(g * GROUP + b, wstage[:, b:b + 1, :], w_h_done)

                    groups(act, stage_group)
                    with act.Fori(0, T) as i:
                        t = i + base
                        act.wait_ge(w_u_done, t + 1)
                        nc.scalar.activation(wUT[:, :], bank(6)[:, 0:P], ACT.Identity, bias=mix_col[:, layer:layer + 1])\
                          .then_inc(w_ut_done, 1)
                        act.wait_ge(w_cbias_done, t + 1)
                        for c in range(WCHUNKS):
                            act.wait_ge(w_s_done, WCHUNKS * t + c + 1)
                            nc.scalar.activation(wS[:, c * WCH:(c + 1) * WCH], wpsS[c % 2], ACT.Identity,
                                                 bias=wcbias[:, 0:1], scale=1.0 if layer == 0 else SCALE).then_inc(w_s_moved, 1)
                        act.wait_ge(w_nmax_done, t + 1)
                        nc.scalar.activation(wS[:, :], wS[:, :], ACT.Exp, bias=wnmax[:, 0:1], accum_out=wrsum[:, 0:1])\
                          .then_inc(w_exp_done, 1)
                        for c in range(WCHUNKS):
                            act.wait_ge(w_p_turned, WCHUNKS * t + c + 1)
                            if c >= 2:
                                act.wait_ge(w_pt_used, WCHUNKS * t + c - 1)
                            nc.scalar.activation(wPT[:, c % 2, :], wpsT[c % 2], ACT.Identity).then_inc(w_pt_done, 1)
                        act.wait_ge(w_zneg_done, t + 1)
                        nc.scalar.activation(wzexp[:, :], wzneg[:, :], ACT.Exp).then_inc(w_zexp_done, 1)
            with act.Else():
                for layer in range(2):
                    base = layer * T
                    if layer:
                        sd_of(2)
                        stage_h()

                    def move_owners(t, b):
                        for u in range(2):
                            half = slice(u * CHUNKS // 2, (u + 1) * CHUNKS // 2)
                            act.wait_ge(turned, 2 * (t + base) + u + 1)
                            for to in (owners, owners16):
                                last_one = nc.scalar.activation(to[:, b % GROUP, half, :].rearrange("p c q -> p (c q)"),
                                                                turned_ps[u], ACT.Identity)
                            last_one.then_inc(owners_done, 1)

                    def move_acc(t, b):
                        tt = t + base
                        act.wait_ge(rsum_done, tt + 1)
                        nc.scalar.activation(acc[:, :], bank(6)[:, 0:P], ACT.Identity, scale=rsum[:, 0:1]).then_inc(acc_sb, 1)
                        act.wait_ge(acc_turned, tt + 1)
                        nc.scalar.activation(accT[:, :], bank(7)[:, 0:P], ACT.Identity).then_inc(accT_sb, 1)

                    def exp_z(t, b):
                        act.wait_ge(zneg_done, t + base + 1)
                        nc.scalar.activation(zexp[:, :], zneg[:, :], ACT.Exp).then_inc(zexp_done, 1)

                    def attend_group(g, first, last):
                        if first:
                            for b in range(3):
                                move_owners(b, b)
                        for b in range(GROUP):
                            t = g * GROUP + b
                            act.wait_ge(below_done, t + base + 1)
                            nc.scalar.activation(prob[:, :], gap[:, :], ACT.Exp).then_inc(prob_done, 1)
                            if not (first and b == 0):
                                move_acc(t - 1, b - 1)
                                exp_z(t - 1, b - 1)
                            if not (last and b >= GROUP - 3):
                                move_owners(t + 3, b + 3)
                        if last:
                            move_acc(t, b)
                            exp_z(t, b)

                    groups(act, attend_group)

        @block.tensor
        def _(pe):
            pe.wait_ge(consts_in, 16 * 9)
            pe.wait_ge(pool_consts, 20 + 2 * GROUP)
            nc.tensor.transpose(bank(0)[:, 0:D], w_sb, ident[:, :]).then_inc(w_turned, 1)
            nc.tensor.transpose(bank(0)[:, D:2 * D], wv_sb, ident[:, :]).then_inc(w_turned, 1)
            pe.wait_ge(w_turned_sb, 1)
            pe.wait_ge(spread_done, 4)
            nc.tensor.matmul(bank(1)[:, 0:1], wT[:, 0, :], a1_c, start=True, stop=True)
            nc.tensor.matmul(bank(1)[:, 1:2], wT[:, 0, :], a2_c, start=True, stop=True)
            nc.tensor.matmul(bank(1)[:, 2:3], wk_sb, bq_c, start=True, stop=True)
            nc.tensor.matmul(bank(1)[:, 128:256], spread[:, 1, :], wT[:, 0, :], start=True, stop=True)
            nc.tensor.matmul(bank(1)[:, 256:384], ones[0:1, 0:P], bvrow[0:1, :], start=True, stop=True)
            nc.tensor.matmul(bank(2)[:, 0:DE], wq_sb, wk_bk[:, :], start=True, stop=True)
            nc.tensor.matmul(bank(3)[:, 0:DE], spread[:, 0, :], wk_bk[:, :], start=True, stop=True).then_inc(mixed, 1)
            pe.wait_ge(mixed_sb, 9)

            def turn_rows(g, k, layer):
                pe.wait_ge(h_done, (g + 1) * GROUP + layer * T)
                for b in range(GROUP):
                    last = nc.tensor.transpose((bank(k) if layer else bank(7))[:, b * P:(b + 1) * P],
                                               stage[:, k, b, :], ident[:, :])
                last.then_inc(h_turned, 1)

            def make_u(k, n, ps, layer):
                for b in range(2):
                    at = (2 * n + b) * P
                    last = nc.tensor.matmul(ps[:, b * 256:b * 256 + DE], stageT[:, k, at:at + P], mix[:, layer, :],
                                            start=True, stop=True)
                return last

            def make_layer():
                def pair(j, first, last):
                    for k in range(2):
                        g = 2 * j + k
                        pe.wait_ge(ht_done, g - 1 + G)
                        turn_rows(g, k, 1)
                        if not (first and k == 0):
                            make(g - 1, (k + 1) % 2)
                    if last:
                        make(g, k)

                def make(g, k):
                    pe.wait_ge(ht_done, g + 1 + G)
                    pe.wait_ge(u_kept, 2 * (g - 1 + G))
                    for n in range(2):
                        last_one = make_u(k, n, bank(2 + 2 * k + n), 1)
                    last_one.then_inc(u_done, 1)

                in_pairs(pe, pair)

            pe.wait_ge(dve_consts, SEGS + 2)

            def pack(g, b, wait_used):
                t = g * GROUP + b
                if wait_used:
                    pe.wait_ge(rest_done, 2 * t - 3)
                pe.wait_ge(mask_done, QUARTERS * (t + 1))
                for s in range(SEGS):
                    for c0, c1 in parts:
                        nc.tensor.matmul(V[b % 2][:, c0:c1], shifted[:, s, :],
                                         mask[:, b % 2, s * BLOCK + c0:s * BLOCK + c1], start=(s == 0), stop=False)
                for n, low in enumerate((place_hi, place_lo)):
                    for c0, c1 in parts:
                        last = nc.tensor.matmul(V[b % 2][:, c0:c1], ones16[0:1, :], low[0:1, c0:c1],
                                                start=False, stop=(n == 1))
                last.then_inc(packed, 1)

            def ends(g):
                pe.wait_ge(count_done, 3 * g + 3)
                nc.tensor.matmul(bank(6)[:, 0:GROUP], upto[:, :], count16[:, :], start=True, stop=True).then_inc(ends_done, 1)

            def deal(g, b):
                t = g * GROUP + b
                if b == 0:
                    pe.wait_ge(split_done, 6 * (g + 1))
                pe.wait_ge(mine_done, 3 * t + 3)
                for c in range(CHUNKS):
                    for part in (hi16, lo16):
                        last = nc.tensor.matmul(q_lists[b % 2][:, c, :], mine[:, b % 2, c * P:(c + 1) * P], part[:, b, :],
                                                start=(part is hi16), stop=(part is lo16))
                last.then_inc(q_done, 1)

            def survey_group(g, first, last):
                for b in range(GROUP):
                    pack(g, b, not (first and b < 2))
                    if not first:
                        if b == 0:
                            ends(g - 1)
                        else:
                            deal(g - 1, b - 1)
                    if b == 2:
                        if not first:
                            pe.wait_ge(u_kept, 2 * g)
                        turn_rows(g, 0, 0)
                    if b == 3:
                        pe.wait_ge(ht_done, g + 1)
                        make_u(0, 0, bank(7), 0).then_inc(u_done, 1)
                if not first:
                    deal(g - 1, GROUP - 1)
                pe.wait_ge(u_kept, 2 * g + 1)
                make_u(0, 1, bank(7), 0).then_inc(u_done, 1)
                if last:
                    ends(g)
                    for b in range(GROUP):
                        deal(g, b)

            groups(pe, survey_group)
            pe.wait_ge(u_kept, 2 * G)
            pe.wait_ge(bad_done, 10)
            nc.tensor.matmul(bank(7)[:, 0:1], ones[:, 0:P], bad_row[:, :], start=True, stop=True).then_inc(bad_summed, 1)

            pe.wait_ge(flag_done, 1)
            whole = pe.value_load(flag[0:1, 0:1], min_val=0, max_val=1)
            with pe.If(whole > 0):
                for layer in range(2):
                    base = layer * T
                    def turn_chunk(i, first):
                        pe.wait_ge(w_h_done, (i + 1) * WTILES + base)
                        if layer or not first:
                            pe.wait_ge(w_ht_done, i + layer * WCHUNKS)
                        for n in range(WTILES):
                            last = nc.tensor.transpose(wpsT[0][:, n * P:(n + 1) * P], wstage[:, n, :], ident[:, :])
                        last.then_inc(w_h_turned, 1)

                    counted(pe, WCHUNKS, turn_chunk)
                    pe.wait_ge(w_ht_done, (layer + 1) * WCHUNKS)
                    pe.wait_ge(w_h_kept, (layer + 1) * WCHUNKS)
                    with pe.Fori(0, T) as i:
                        t = i + base
                        pe.wait_ge(w_rows_done, t + 1)
                        nc.tensor.matmul(bank(6)[:, 0:P], mix[:, layer, 0:D], wrows[:, :], start=True, stop=True)
                        nc.tensor.matmul(bank(7)[:, 0:1], wrows[:, :], mix[:, layer, D:DE], start=True, stop=True)\
                          .then_inc(w_u_done, 1)
                        pe.wait_ge(w_ut_done, t + 1)
                        for c in range(WCHUNKS):
                            if c >= 2:
                                pe.wait_ge(w_s_moved, WCHUNKS * t + c - 1)
                            nc.tensor.matmul(wpsS[c % 2], wUT[:, :], wHT[:, c * WCH:(c + 1) * WCH], start=True, stop=True)\
                              .then_inc(w_s_done, 1)
                        pe.wait_ge(w_exp_done, t + 1)

                        def weigh(c):
                            pe.wait_ge(w_pt_done, WCHUNKS * t + c + 1)
                            for n in range(WTILES):
                                last = nc.tensor.matmul(bank(4)[:, 0:P], wH[:, c * WTILES + n, :],
                                                        wPT[:, c % 2, n * P:(n + 1) * P], start=(c == 0 and n == 0),
                                                        stop=(c == WCHUNKS - 1 and n == WTILES - 1))
                            last.then_inc(w_pt_used, 1)

                        for c in range(WCHUNKS):
                            if c >= 2:
                                pe.wait_ge(w_pt_done, WCHUNKS * t + c - 1)
                            for n in range(WTILES):
                                at = c * WCH + n * P
                                last = nc.tensor.transpose(wpsT[c % 2][:, n * P:(n + 1) * P], wS[:, at:at + P], ident[:, :])
                            last.then_inc(w_p_turned, 1)
                            if c >= 1:
                                weigh(c - 1)
                        weigh(WCHUNKS - 1)
                        pe.wait_ge(w_pt_used, WCHUNKS * t + WCHUNKS)
                        pe.sem_inc(w_a_done, 1)
                        pe.wait_ge(w_at_done, t + 1)
                        nc.tensor.matmul(bank(5)[:, 0:D], wAT[:, :], proj[:, layer, :], start=True, stop=True)\
                          .then_inc(w_o_done, 1)
            with pe.Else():
                for layer in range(2):
                    base = layer * T
                    if layer:
                        make_layer()
                    pe.wait_ge(u_kept, 2 * G * (layer + 1))

                    def turn(t, b):
                        tt = t + base
                        pe.wait_ge(owned_done, tt + 1)
                        for u in range(2):
                            if not (layer == 0 and isinstance(t, int) and t == 0):
                                pe.wait_ge(owners_done, 2 * tt + u - 1)
                            for n in range(CHUNKS // 2):
                                last = nc.tensor.transpose(turned_ps[u][:, n * P:(n + 1) * P],
                                                           owned[:, b % GROUP, u * CHUNKS // 2 + n, :], ident16[:, :])
                            last.then_inc(turned, 1)

                    def spread_part(t, b, u):
                        for c in range(*spread_parts[u]):
                            last = nc.tensor.matmul(spread_ps[u][:, c - spread_parts[u][0], :],
                                                    owners[:, b % GROUP, c, :],
                                                    U[:, bass.ds(t, 1), :].rearrange("p o d -> p (o d)"),
                                                    start=True, stop=True)
                        return last

                    def spread_rows(t, b, skip):
                        tt = t + base
                        pe.wait_ge(owners_done, 2 * tt + 2)
                        for u in range(SPREADS - 1):
                            if not skip:
                                pe.wait_ge(prod_done, SPREADS * (tt - 1) + u + 1)
                            spread_part(t, b, u).then_inc(spread_u, 1)

                    def turn_acc(t, b):
                        tt = t + base
                        pe.wait_ge(acc_sb, tt + 1)
                        pe.wait_ge(z_done, tt)
                        nc.tensor.transpose(bank(7)[:, 0:P], acc[:, :], ident[:, :]).then_inc(acc_turned, 1)

                    def project(t, b):
                        tt = t + base
                        pe.wait_ge(accT_sb, tt + 1)
                        nc.tensor.matmul(bank(7)[:, 0:D], accT[:, :], proj[:, layer, :], start=True, stop=True)\
                          .then_inc(o_done, 1)

                    def scatter(t, b, next_too):
                        pe.wait_ge(slot_e_done, t + base + 1)
                        for c in range(CHUNKS):
                            for n in range(2):
                                last = nc.tensor.matmul(by_slot_ps, owned[:, b % GROUP, c, :], slot_e[:, n, c, :],
                                                        start=(c == 0 and n == 0), stop=(c == CHUNKS - 1 and n == 1))
                        if next_too:
                            last = spread_part(t + 1, b + 1, SPREADS - 1)
                        last.then_inc(scattered, 1)

                    def spread_max(t, b):
                        pe.wait_ge(max_done, 3 * (t + base) + 3)
                        for c in range(CHUNKS):
                            for n in range(2):
                                last = nc.tensor.matmul(max_ps[:, c:c + 1], owners16[:, b % GROUP, c, :], max16[:, n:n + 1],
                                                        start=(n == 0), stop=(n == 1))
                        last.then_inc(max_spread, 1)

                    def sum_up(t, b):
                        tt = t + base
                        pe.wait_ge(weighted_done, tt + 1)
                        pe.wait_ge(acc_sb, tt)
                        for c in range(CHUNKS):
                            last = nc.tensor.matmul(bank(6)[:, 0:DE], weighted[:, b % 2, c, :], Gt[:, b, c, :],
                                                    start=(c == 0), stop=(c == CHUNKS - 1))
                        last.then_inc(acc_done, 1)

                    def attend_group(g, first, last):
                        if first:
                            for b in range(3):
                                turn(b, b)
                            spread_rows(0, 0, layer == 0)
                            spread_part(0, 0, SPREADS - 1).then_inc(scattered, 1)
                            spread_rows(1, 1, False)
                            scatter(0, 0, True)
                            spread_max(0, 0)
                        for b in range(GROUP):
                            t = g * GROUP + b
                            before = not (first and b == 0)
                            after = not (last and b == GROUP - 1)
                            after2 = not (last and b >= GROUP - 2)
                            if after2:
                                spread_rows(t + 2, b + 2, False)
                            if after:
                                scatter(t + 1, b + 1, after2)
                            if before:
                                turn_acc(t - 1, b - 1)
                                project(t - 1, b - 1)
                            if not (last and b >= GROUP - 3):
                                turn(t + 3, b + 3)
                            if after:
                                spread_max(t + 1, b + 1)
                            sum_up(t, b)
                        if last:
                            turn_acc(t, b)
                            project(t, b)

                    groups(pe, attend_group)


_INS = ['x', 'adj', 'L0_gnn_W', 'L0_gnn_a', 'L1_gnn_Wq', 'L1_gnn_bq', 'L1_gnn_Wk', 'L1_gnn_bk', 'L1_gnn_Wv', 'L1_gnn_bv']
_OUTS = [((8192, 128), 'float32')]


def kernel(**inputs):
    import numpy as _np
    import concourse.bacc as _bacc
    from concourse import mybir as _mybir
    from concourse.bass_utils import run_bass_kernel_spmd as _run

    nc = _bacc.Bacc("TRN2", target_bir_lowering=False, num_devices=1)
    arrays, args = {}, []
    for name in _INS:
        a = _np.ascontiguousarray(inputs[name])
        arrays[f"in_{name}_dram"] = a
        args.append(nc.dram_tensor(f"in_{name}_dram", a.shape, _mybir.dt.from_np(a.dtype), kind="ExternalInput").ap())
    for i, (shape, dtype) in enumerate(_OUTS):
        dt = _mybir.dt.from_np(_np.dtype(dtype))
        args.append(nc.dram_tensor(f"out_{i}_dram", shape, dt, kind="ExternalOutput").ap())
    two_layer_graph_attention(nc, *args)
    r = _run(nc, [arrays], core_ids=[0])
    return r.results[0]["out_0_dram"]
```
